# Optimizing a Trainium2 kernel written in Bass

```python
import numpy as np
import jax
import jax.numpy as jnp

def _softmax(x, axis=-1):
    return jax.nn.softmax(x, axis=axis)

def _gelu(x):
    return jax.nn.gelu(x, approximate=True)

def _silu(x):
    return jax.nn.silu(x)

def _sigmoid(x):
    return jax.nn.sigmoid(x)

def _layernorm(x, axis=-1, eps=1e-05):
    m = jnp.mean(x, axis=axis, keepdims=True)
    v = jnp.var(x, axis=axis, keepdims=True)
    return (x - m) / jnp.sqrt(v + eps)

def _scatter_add(tgt, idx, src, axis=0):
    return tgt.at[idx].add(src)

def _segment_sum(src, seg, n):
    return jax.ops.segment_sum(src, seg, n)
kernel_name = 'mk_adj_preln_d2_adj_r2_6b5831'

def setup_inputs(seed: int=0):
    np.random.seed(seed)
    _w = jnp.asarray

    def _rec_inputs():
        import jax
        import jax.numpy as jnp
        _gk = jax.random.key(seed)
        x = -0.0002928 + 1 * jax.random.normal(jax.random.fold_in(_gk, 1), (128, 128, 256), jnp.float32)
        _a = jax.random.bernoulli(jax.random.fold_in(_gk, 2), 0.03125, (128, 128, 128))
        adj = _a.astype(jnp.int32)
        return (x, adj)
    x, adj = _rec_inputs()

    def _L0_gnn_setup():
        import jax, jax.numpy as jnp
        import numpy as np
        ALPHA = 0.2
        K_NUM = 16
        NEG_INF = -9000000000000000.0
        key = jax.random.key(seed)
        k1, k2, k3, k4 = jax.random.split(key, 4)
        B, N, F_in, F_out = (4, 1024, 256, 256)
        h = jax.random.normal(k1, (B, N, F_in), dtype=jnp.float32)
        adj = jax.random.randint(k2, (B, N, N), 0, 2, dtype=jnp.int32)

        def xavier(k, shape, gain=1.414):
            fan_in, fan_out = (shape[0], shape[1])
            bound = gain * np.sqrt(6.0 / (fan_in + fan_out))
            return jax.random.uniform(k, shape, jnp.float32, -bound, bound)
        W = xavier(k3, (F_in, F_out))
        a = xavier(k4, (2 * F_out, 1))
        return {'h': h, 'adj': adj, 'W': W, 'a': a}
    _L0_gnn_all = _L0_gnn_setup()
    _L0_gnn_in = {k: v for k, v in _L0_gnn_all.items() if k in ('W', 'a')}
    del _L0_gnn_all

    def _L1_gnn_setup():
        import jax, jax.numpy as jnp
        import numpy as np
        L = 3
        D = 256
        B, N = (8, 512)
        EPS = 1e-05

        def layernorm(x, gamma, beta):
            mu = jnp.mean(x, axis=-1, keepdims=True)
            var = jnp.var(x, axis=-1, keepdims=True)
            return (x - mu) * jax.lax.rsqrt(var + EPS) * gamma + beta
        key = jax.random.key(seed)
        ks = jax.random.split(key, 12)
        s = 1.0 / np.sqrt(D)
        node_features = jax.random.normal(ks[0], (B, N, D), dtype=jnp.float32)
        adjacency_matrix = jax.random.randint(ks[1], (B, N, N), 0, 2, dtype=jnp.int32)
        return {'node_features': node_features, 'adjacency_matrix': adjacency_matrix, 'attn_w': jax.random.normal(ks[2], (L, 2 * D), dtype=jnp.float32) * (1.0 / np.sqrt(2 * D)), 'attn_b': jax.random.normal(ks[3], (L,), dtype=jnp.float32) * 0.01, 'W1': jax.random.normal(ks[4], (L, D, 4 * D), dtype=jnp.float32) * s, 'b1': jnp.zeros((L, 4 * D), dtype=jnp.float32), 'W2': jax.random.normal(ks[5], (L, 4 * D, D), dtype=jnp.float32) * (1.0 / np.sqrt(4 * D)), 'b2': jnp.zeros((L, D), dtype=jnp.float32), 'g1': jnp.ones((L, D), dtype=jnp.float32), 'beta1': jnp.zeros((L, D), dtype=jnp.float32), 'g2': jnp.ones((L, D), dtype=jnp.float32), 'beta2': jnp.zeros((L, D), dtype=jnp.float32)}
    _L1_gnn_all = _L1_gnn_setup()
    _L1_gnn_in = {k: v for k, v in _L1_gnn_all.items() if k in ('attn_w', 'attn_b', 'W1', 'b1', 'W2', 'b2', 'g1', 'beta1', 'g2', 'beta2')}
    del _L1_gnn_all
    return {'x': x, 'adj': adj, 'L0_gnn_W': _L0_gnn_in['W'], 'L0_gnn_a': _L0_gnn_in['a'], 'L1_gnn_attn_w': _L1_gnn_in['attn_w'], 'L1_gnn_attn_b': _L1_gnn_in['attn_b'], 'L1_gnn_W1': _L1_gnn_in['W1'], 'L1_gnn_b1': _L1_gnn_in['b1'], 'L1_gnn_W2': _L1_gnn_in['W2'], 'L1_gnn_b2': _L1_gnn_in['b2'], 'L1_gnn_g1': _L1_gnn_in['g1'], 'L1_gnn_beta1': _L1_gnn_in['beta1'], 'L1_gnn_g2': _L1_gnn_in['g2'], 'L1_gnn_beta2': _L1_gnn_in['beta2']}

def reference(x, adj, L0_gnn_W, L0_gnn_a, L1_gnn_attn_w, L1_gnn_attn_b, L1_gnn_W1, L1_gnn_b1, L1_gnn_W2, L1_gnn_b2, L1_gnn_g1, L1_gnn_beta1, L1_gnn_g2, L1_gnn_beta2):
    import jax
    import jax.numpy as jnp

    def _L0_gnn_ref(h, adj, W, a):
        import jax, jax.numpy as jnp
        import numpy as np
        ALPHA = 0.2
        K_NUM = 16
        NEG_INF = -9000000000000000.0
        F_out = W.shape[1]
        Wh = jnp.einsum('bnf,fo->bno', h, W)
        a1, a2 = (a[:F_out, 0], a[F_out:, 0])
        e_src = Wh @ a1
        e_dst = Wh @ a2
        e = e_src[:, :, None] + e_dst[:, None, :]
        e = jnp.where(e > 0, e, ALPHA * e)
        e = jnp.where(adj > 0, e, NEG_INF)
        attention = jax.nn.softmax(e, axis=2)
        topk_vals = jax.lax.top_k(attention, K_NUM)[0]
        kth = topk_vals[:, :, -1:]
        attention = jnp.where(attention < kth, 0.0, attention)
        h_prime = jnp.einsum('bij,bjo->bio', attention, Wh)
        return jax.nn.elu(h_prime)

    def _L1_gnn_ref(node_features, adjacency_matrix, attn_w, attn_b, W1, b1, W2, b2, g1, beta1, g2, beta2):
        import jax, jax.numpy as jnp
        import numpy as np
        L = 3
        D = 256
        B, N = (8, 512)
        EPS = 1e-05

        def layernorm(x, gamma, beta):
            mu = jnp.mean(x, axis=-1, keepdims=True)
            var = jnp.var(x, axis=-1, keepdims=True)
            return (x - mu) * jax.lax.rsqrt(var + EPS) * gamma + beta
        n = adjacency_matrix.shape[-1]
        mask = adjacency_matrix.astype(jnp.float32) + jnp.eye(n, dtype=jnp.float32) > 0
        x = node_features
        d = x.shape[-1]
        for l in range(attn_w.shape[0]):
            si = x @ attn_w[l, :d]
            sj = x @ attn_w[l, d:]
            scores = si[:, :, None] + sj[:, None, :] + attn_b[l]
            scores = jnp.where(scores >= 0, scores, 0.2 * scores)
            scores = jnp.where(mask, scores, -jnp.inf)
            attn = jax.nn.softmax(scores, axis=-1)
            agg = jnp.einsum('bij,bjd->bid', attn, x)
            h = layernorm(x + agg, g1[l], beta1[l])
            ff = jax.nn.gelu(h @ W1[l] + b1[l], approximate=False) @ W2[l] + b2[l]
            x = layernorm(h + ff, g2[l], beta2[l])
        return x
    h = jnp.maximum(_layernorm(x, axis=-1), 0.0)
    x = x + _L0_gnn_ref(h, adj, L0_gnn_W, L0_gnn_a)
    h = jnp.maximum(_layernorm(x, axis=-1), 0.0)
    x = x + _L1_gnn_ref(h, adj, L1_gnn_attn_w, L1_gnn_attn_b, L1_gnn_W1, L1_gnn_b1, L1_gnn_W2, L1_gnn_b2, L1_gnn_g1, L1_gnn_beta1, L1_gnn_g2, L1_gnn_beta2)
    return x

_drawn_inputs = setup_inputs


def setup_inputs(seed=0):
    import zlib

    import numpy as np

    out = dict(_drawn_inputs(seed))
    spreads = {'L1_gnn_b1': (0.0, 0.1),
     'L1_gnn_b2': (0.0, 0.1),
     'L1_gnn_g1': (1.0, 0.2),
     'L1_gnn_beta1': (0.0, 0.1),
     'L1_gnn_g2': (1.0, 0.2),
     'L1_gnn_beta2': (0.0, 0.1)}
    factors = {'L1_gnn_attn_b': 193.102}
    for name, (base, spread) in spreads.items():
        noise = np.random.default_rng([zlib.crc32(name.encode()), seed]).standard_normal(out[name].shape)
        drawn = base * np.exp(spread * noise) if base else spread * noise
        out[name] = jnp.asarray(drawn.astype(out[name].dtype))
    for name, factor in factors.items():
        out[name] = (out[name] * factor).astype(out[name].dtype)
    return out
```

```python
from contextlib import ExitStack

import concourse.bass as bass
from concourse import mybir

F32 = mybir.dt.float32
F32R = mybir.dt.float32r
BF16 = mybir.dt.bfloat16
I32 = mybir.dt.int32
ALU = mybir.AluOpType
ACT = mybir.ActivationFunctionType

P = 128
D = 256
G = 4
B = 128
NG = B // G
L = 3
HID = 4 * D
MC = HID // P
DC = D // P
TOPK_ROUNDS = 2
EPS = 1e-5
SLOPE = 0.2
OFF = -2.0 ** 100
FIRST_STEADY, LAST_STEADY = 3, NG - 3


class At:

    def __init__(self, i, a, b):
        self.i, self.a, self.b = i, a, b

    def __add__(self, c):
        return At(self.i, self.a, self.b + c)

    def __sub__(self, c):
        return self + (-c)

    def __mul__(self, c):
        return At(self.i, self.a * c, self.b * c)

    def value(self):
        return self.i * self.a + self.b


def value(n):
    return n.value() if isinstance(n, At) else n


def here(k):
    return isinstance(k, At) or 0 <= k < NG


def seq(k, l):
    if isinstance(k, At):
        return k * L + ((L + 1) * l - L)
    at = L * k + (L + 1) * l
    return sum(L * kk + (L + 1) * ll < at for kk in range(NG) for ll in range(L))


def wait(eng, sem, n):
    if isinstance(n, At):
        eng.wait_ge(sem, n.value())
    elif n > 0:
        eng.wait_ge(sem, n)


def build_program(nc, x, adj, W0, a0, attn_w, attn_b, W1, b1, W2, b2, g1, be1, g2, be2, out):
    ctx = ExitStack()
    with ctx:
        def sb(name, shape, dt=F32):
            return ctx.enter_context(nc.sbuf_tensor(name, [P] + shape, dt))

        def bank(name):
            return ctx.enter_context(nc.psum_tensor(name, [P, 512], F32))

        def sem(name):
            return ctx.enter_context(nc.semaphore(name))

        w1_hi = sb("w1_hi", [L, DC, HID], F32R)
        w1_lo = sb("w1_lo", [L, DC, HID], F32R)
        w2_sb = sb("w2_sb", [L, MC, D])
        w0_hi = sb("w0_hi", [DC, D], F32R)
        w0_lo = sb("w0_lo", [DC, D], F32R)
        a0_row = sb("a0_row", [2, D])
        wij_row = sb("wij_row", [L, 2, D])
        b_att = sb("b_att", [L])
        g1_row = sb("g1_row", [L, D])
        bb_row = sb("bb_row", [L, D])
        g2_row = sb("g2_row", [L, D])
        be2_row = sb("be2_row", [L, D])
        g1_col = sb("g1_col", [L, DC])
        be1_col = sb("be1_col", [L, DC])
        b1_col = sb("b1_col", [L, MC])
        ident = sb("ident", [P])
        minus_half = sb("minus_half", [G])

        X = sb("X", [L, G, D])
        H = sb("H", [L, G, D])
        ht_hi = sb("ht_hi", [L, DC, G * P], F32R)
        ht_lo = sb("ht_lo", [L, DC, G * P], F32R)
        ht_f = sb("ht_f", [G * P])
        Y = sb("Y", [G, D])
        x1 = sb("x1", [G, D])
        adj_sb = sb("adj_sb", [G, P], I32)
        mask0 = sb("mask0", [G, P], BF16)
        mask_out = sb("mask_out", [G, P], BF16)
        mask_in = sb("mask_in", [L, G, P], BF16)
        U = sb("U", [G, P])
        EB = sb("EB", [G, P])
        pt_hi = sb("pt_hi", [G * P], F32R)
        pt_lo = sb("pt_lo", [G * P], F32R)
        x_hi = sb("x_hi", [G, D], F32R)
        x_lo = sb("x_lo", [G, D], F32R)
        A = sb("A", [4, G * P])
        hn0 = sb("hn0", [G, D])
        h0_hi = sb("h0_hi", [DC, 2 * P], F32R)
        h0_lo = sb("h0_lo", [DC, 2 * P], F32R)
        wh_hi = sb("wh_hi", [G, D], F32R)
        wh_lo = sb("wh_lo", [G, D], F32R)
        U0 = sb("U0", [G, P])
        EB0 = sb("EB0", [G, P])
        pt0_hi = sb("pt0_hi", [G * P], F32R)
        pt0_lo = sb("pt0_lo", [G * P], F32R)
        junk = sb("junk", [8, D], BF16)

        def stats_of(name):
            return dict(six=sb(name + "_six", [G, 6]), mv=sb(name + "_mv", [G, 2]), ve=sb(name + "_ve", [G]),
                        rstd=sb(name + "_rstd", [G]), nmr=sb(name + "_nmr", [G]))

        stats = {n: stats_of("st_" + n) for n in ("x", "r", "h", "y")}
        sij = sb("sij", [L, 2, G])
        sib = sb("sib", [L, G])
        smax, ssum, smx, bias_a, bias_b, den, rden = (
            sb("a_" + n, [G]) for n in ("smax", "ssum", "smx", "bias_a", "bias_b", "den", "rden"))
        e0 = sb("e0", [2, G])
        zmax, zsum, zmx, zbias_a, zbias_b, zden, zrden = (
            sb("z_" + n, [G]) for n in ("smax", "ssum", "smx", "bias_a", "bias_b", "den", "rden"))
        top = sb("top", [TOPK_ROUNDS, G, 8])
        kept = sb("kept", [G, P])

        ps_mm = [bank("ps_mm0"), bank("ps_mm1")]
        ps_ff = [bank("ps_ff0"), bank("ps_ff1")]
        ps_s, ps_ag, ps_ht, ps_0 = bank("ps_s"), bank("ps_ag"), bank("ps_ht"), bank("ps_0")

        mask_park = nc.dram_tensor("mask_park", [NG, P, G * P], BF16, kind="Internal").ap()

        s = {}
        for name in (
            "const_in", "w0_in", "w1_in", "w2_in", "const_made", "ident_zero", "w1_split", "w0_split", "hold_vector", "hold_sync",
            "hold_pool", "x_in", "adj_in", "mask_parked", "mask_made", "adj_sum", "x1_out", "out_added",
            "xst_six", "xst_mv", "xst_ve", "xst_rstd", "xst_nmr", "x_norm",
            "h0_turned", "h0_hi_made", "h0_split", "wh_made", "wh_hi_made", "wh_split", "e0_made",
            "e0_turned", "z_scored", "z_summed", "z_maxed", "z_biased", "z_exped", "z_probs", "z_top1", "z_rest", "z_top2",
            "z_kept", "z_turned", "z_hi_made", "z_split", "z_agg", "z_rden_made", "elu_exped", "elu_relu", "elu_sum", "x1_made",
            "rst_six", "rst_mv", "rst_ve", "rst_rstd", "rst_nmr",
            "sij_made", "sib_made", "sj_turned", "scored", "summed", "maxed", "biased", "exped", "probs", "p_turned",
            "p_hi_made", "p_split", "x_hi_made", "x_lo_made", "agg_made", "rden_made", "y1_made",
            "hst_six", "hst_mv", "hst_ve", "hst_rstd", "hst_nmr", "h_norm", "h_turned", "ht_f_made", "ht_hi_made", "ht_split",
            "h_scaled", "h_res", "mm1_made", "gelu_made", "mm2_made",
            "y_made", "yst_six", "yst_mv", "yst_ve", "yst_rstd", "yst_nmr", "y_norm", "y_scaled", "y_final",
        ):
            s[name] = sem(name)
        s_x = [sem(f"x_ready{l}") for l in range(L)]
        s_mask = [sem(f"mask_in{l}") for l in range(L)]

        x_g = x.rearrange("(k g) n d -> k n g d", g=G)
        adj_g = adj.rearrange("(k g) n m -> k n g m", g=G)
        out_g = out.rearrange("(k g) n d -> k n g d", g=G)

        CONSTS = 10
        STAGED = 2
        LOADS0 = 16

        def row(ap, n):
            return ap.rearrange("(o n) -> o n", o=1).to_broadcast([P, n])

        def schedule(iteration, eng):
            for i in range(-2, FIRST_STEADY):
                iteration(i)
            with eng.Fori(FIRST_STEADY, LAST_STEADY + 1) as i:
                iteration(At(i, 1, 0))
            for i in range(LAST_STEADY + 1, NG + L):
                iteration(i)

        def slots(i):
            for t in range(L):
                yield (t, [(i + (1 - t), t), (i + (-2, 1, 0)[t], (2, 0, 1)[t]), (i + (-1, -2, 1)[t], (1, 2, 0)[t]),
                           (i - t, t), (i + (-3, 0, -1)[t], (2, 0, 1)[t])])

        block = ctx.enter_context(nc.Block())

        @block.sync
        def _(sp):
            sp.dma_start(Y[:, 0:DC, :], W0.rearrange("(c p) n -> p c n", p=P)).then_inc(s["w0_in"], 16)
            sp.dma_start(X[:, 0:2, :, :].rearrange("p l g d -> p (l g d)"),
                         W1[0].rearrange("(c p) n -> p c n", p=P)).then_inc(s["w1_in"], 16)
            for t, src in ((a0_row, row(a0.rearrange("n o -> (n o)"), 2 * D)), (wij_row, row(attn_w.rearrange("l n -> (l n)"), L * 2 * D)),
                           (b_att, row(attn_b, L)), (g1_row, row(g1.rearrange("l n -> (l n)"), L * D)),
                           (bb_row, row(be1.rearrange("l n -> (l n)"), L * D)), (g2_row, row(g2.rearrange("l n -> (l n)"), L * D)),
                           (be2_row, row(be2.rearrange("l n -> (l n)"), L * D))):
                shape = "p a b -> p (a b)" if len(t.shape) == 3 else "p a b c -> p (a b c)"
                dst = t[:] if len(t.shape) == 2 else t[:].rearrange(shape)
                sp.dma_start(dst, src).then_inc(s["const_in"], 16)
            with nc.allow_non_contiguous_dma(reason="three short columns, once"):
                sp.dma_start(g1_col[:], g1.rearrange("l (c p) -> p l c", p=P)).then_inc(s["const_in"], 16)
                sp.dma_start(be1_col[:], be1.rearrange("l (c p) -> p l c", p=P)).then_inc(s["const_in"], 16)
                sp.dma_start(b1_col[:], b1.rearrange("l (c p) -> p l c", p=P)).then_inc(s["const_in"], 16)
            sp.dma_start(H[:, 2, 0:L, :].rearrange("p g d -> p (g d)"),
                         row(b2.rearrange("l n -> (l n)"), L * D)).then_inc(s["const_in"], 16)
            sp.dma_start(w2_sb[:].rearrange("p l c n -> p (l c) n"),
                         W2.rearrange("l (c p) n -> p (l c) n", p=P)).then_inc(s["w2_in"], 16)
            for l in range(1, L):
                sp.wait_ge(s["w1_split"], l)
                sp.dma_start(X[:, 0:2, :, :].rearrange("p l g d -> p (l g d)"),
                             W1[l].rearrange("(c p) n -> p c n", p=P)).then_inc(s["w1_in"], 16)
            sp.wait_ge(s["w1_split"], L)

            def settle(sem, n):
                wait(sp, sem, n)
                if isinstance(n, At):
                    sp.sem_inc(s["hold_sync"], 1)

            def load_x(k):
                if not here(k):
                    return
                settle(s_x[0], k)
                settle(s["x1_out"], k * 16)
                sp.dma_start(x1[:], x_g[value(k)]).then_inc(s["x_in"], 16)

            def load_adj(k):
                if not here(k):
                    return
                settle(s["mask_made"], k * 2)
                sp.dma_start(adj_sb[:], adj_g[value(k)]).then_inc(s["adj_in"], 16)

            def park_mask(k):
                if not here(k):
                    return
                settle(s["mask_made"], k * 2 + 2)
                sp.dma_start(mask_park[value(k)], mask_out[:].rearrange("p g m -> p (g m)")).then_inc(s["mask_parked"], 16)

            def store_x1(k):
                if not here(k):
                    return
                settle(s["x1_made"], k + 1)
                sp.dma_start(out_g[value(k)], x1[:]).then_inc(s["x1_out"], 16)

            def load_mask(k, l):
                if not here(k):
                    return
                settle(s["mask_parked"], k * 16 + 16)
                if not (isinstance(k, int) and k == 0):
                    settle(s["scored"], seq(k - 1, l) + 1)
                sp.dma_start(mask_in[:, l].rearrange("p g m -> p (g m)"), mask_park[value(k)]).then_inc(s_mask[l], 16)

            def iteration(i):
                store_x1(i + 1)
                load_mask(i + 1, 0)
                load_mask(i, 1)
                load_mask(i - 2, 2)
                load_x(i + 2)
                load_adj(i + 2)
                park_mask(i + 2)

            schedule(iteration, sp)
            sp.wait_ge(s["out_added"], 16 * NG)
            sp.wait_ge(s["x1_out"], 16 * NG)

        @block.gpsimd
        def _(pool):
            pool.memset(ident[:], 0.0).then_inc(s["ident_zero"], 1)
            pool.wait_ge(s["ident_zero"], 1)
            pool.affine_select(out=ident[:], in_=ident[:], compare_op=ALU.not_equal, fill=1.0, base=0,
                               pattern=[[-1, P]], channel_multiplier=1).then_inc(s["const_made"], 1)
            pool.memset(minus_half[:], -0.5).then_inc(s["const_made"], 1)
            pool.wait_ge(s["const_made"], 2)

            def rstd(name, n):
                st, short = stats[name], name + "st_"
                wait(pool, s[short + "ve"], n + 1)
                pool.tensor_tensor(st["rstd"][:], st["ve"][:], minus_half[:], ALU.pow).then_inc(s[short + "rstd"], 1)

            def x_low(k, l):
                n = seq(k, l)
                wait(pool, s["x_hi_made"], n + 1)
                wait(pool, s["agg_made"], n * 2)
                pool.tensor_tensor(x_lo[:], X[:, l], x_hi[:].bitcast(F32), ALU.subtract).then_inc(s["x_lo_made"], 1)

            def h_scale(k, l):
                n = seq(k, l)
                wait(pool, s["h_norm"], n + 1)
                if not (isinstance(k, int) and k == 0):
                    wait(pool, s["y_made"], seq(k - 1, l) + 1)
                pool.tensor_tensor(H[:, l], X[:, l], g1_row[:, l:l + 1, :].to_broadcast([P, G, D]),
                                   ALU.mult).then_inc(s["h_scaled"], 1)

            def y_scale(k, l):
                n = seq(k, l)
                wait(pool, s["y_norm"], n + 1)
                pool.tensor_tensor(Y[:], Y[:], g2_row[:, l:l + 1, :].to_broadcast([P, G, D]),
                                   ALU.mult).then_inc(s["y_scaled"], 1)

            def add_out(k):
                wait(pool, s["y_final"], k + 1)
                if isinstance(k, At):
                    pool.sem_inc(s["hold_pool"], 1)
                wait(pool, s["x1_out"], k * 16 + 16)
                if isinstance(k, At):
                    pool.sem_inc(s["hold_pool"], 1)
                pool.dma_start(out_g[value(k)], Y[:], accum_op=ALU.add).then_inc(s["out_added"], 16)

            def iteration(i):
                for t, (pre, att, mid, ffn, post) in slots(i):
                    if t == 1 and here(i + 2):
                        rstd("x", i + 2)
                    if here(att[0]):
                        x_low(*att)
                    if here(mid[0]):
                        h_scale(*mid)
                    if here(post[0]):
                        rstd("y", seq(*post))
                    if t == 0 and here(pre[0]):
                        rstd("r", pre[0])
                    if here(post[0]):
                        y_scale(*post)
                        if t == 0:
                            add_out(post[0])
                    if here(att[0]):
                        rstd("h", seq(*att))

            schedule(iteration, pool)

        @block.scalar
        def _(act):
            act.wait_ge(s["const_in"], 16 * 11)
            act.wait_ge(s["w0_split"], 1)
            act.wait_ge(s["w1_split"], L + 1)

            def gelu(k, l, m):
                c = seq(k, l) * MC + m
                wait(act, s["mm1_made"], c + 1)
                wait(act, s["mm2_made"], c - 3)
                act.activation(A[:, m % 4], ps_mm[m % 2][:], ACT.Gelu, bias=b1_col[:, l, m:m + 1]).then_inc(s["gelu_made"], 1)

            def norm(name, short, n, dst, src, func, done, free=()):
                st = stats[name]
                wait(act, s[short + "nmr"], n + 1)
                for sem_, v in free:
                    wait(act, sem_, v)
                for g in range(G):
                    last = act.activation(dst(g), src(g), func, bias=st["nmr"][:, g:g + 1], scale=st["rstd"][:, g:g + 1])
                last.then_inc(done, 1)

            def y_norm(k, l):
                norm("y", "yst_", seq(k, l), lambda g: Y[:, g], lambda g: Y[:, g], ACT.Identity, s["y_norm"])

            def h_norm(k, l):
                norm("h", "hst_", seq(k, l), lambda g: X[:, l, g], lambda g: X[:, l, g], ACT.Identity, s["h_norm"])

            def r_norm(k):
                free = () if isinstance(k, int) and k == 0 else (
                    (s["h_turned"], seq(k - 1, 0) * 2 + 2), (s["h_scaled"], seq(k - 1, 0) + 1))
                norm("r", "rst_", k, lambda g: X[:, 0, g], lambda g: x1[:, g], ACT.Relu, s_x[0], free)

            def x0_norm(k):
                wait(act, s["x1_made"], k)
                norm("x", "xst_", k, lambda g: hn0[:, g], lambda g: x1[:, g], ACT.Identity, s["x_norm"])

            def x_high(k, l):
                n = seq(k, l)
                wait(act, s_x[l], k + 1)
                wait(act, s["agg_made"], n * 2)
                act.activation(x_hi[:], X[:, l], ACT.Copy).then_inc(s["x_hi_made"], 1)

            def exps(k, l):
                n = seq(k, l)
                wait(act, s["biased"], n + 1)
                wait(act, s["probs"], n)
                for g in range(G):
                    act.activation(EB[:, g], U[:, g], ACT.Exp, bias=bias_b[:, g:g + 1], scale=SLOPE)
                for g in range(G):
                    last = act.activation(U[:, g], U[:, g], ACT.Exp, bias=bias_a[:, g:g + 1])
                last.then_inc(s["exped"], 1)

            def p_high(k, l):
                n = seq(k, l)
                wait(act, s["p_turned"], n + 1)
                wait(act, s["agg_made"], n * 2)
                act.activation(pt_hi[:], ps_s[:], ACT.Copy).then_inc(s["p_hi_made"], 1)

            def ht_affine(k, l, d):
                n = seq(k, l) * 2 + d
                wait(act, s["h_turned"], n + 1)
                wait(act, s["ht_split"], n)
                act.activation(ht_f[:], ps_ht[:], ACT.Identity, bias=be1_col[:, l, d:d + 1],
                               scale=g1_col[:, l, d:d + 1]).then_inc(s["ht_f_made"], 1)

            def h0_high(k, half):
                n = k * 2 + half
                wait(act, s["h0_turned"], n + 1)
                wait(act, s["wh_made"], n)
                act.activation(h0_hi[:].rearrange("p c n -> p (c n)"), ps_0[:], ACT.Relu).then_inc(s["h0_hi_made"], 1)

            def wh_high(k, half):
                n = k * 2 + half
                wait(act, s["wh_made"], n + 1)
                wait(act, s["e0_made"], n + 1)
                wait(act, s["z_agg"], k * 2)
                act.activation(wh_hi[:, 2 * half:2 * half + 2].rearrange("p g d -> p (g d)"), ps_0[:],
                               ACT.Copy).then_inc(s["wh_hi_made"], 1)

            def z_exps(k):
                wait(act, s["z_biased"], k + 1)
                for g in range(G):
                    act.activation(EB0[:, g], U0[:, g], ACT.Exp, bias=zbias_b[:, g:g + 1], scale=SLOPE)
                for g in range(G):
                    last = act.activation(U0[:, g], U0[:, g], ACT.Exp, bias=zbias_a[:, g:g + 1])
                last.then_inc(s["z_exped"], 1)

            def z_high(k):
                wait(act, s["z_turned"], k + 1)
                wait(act, s["z_agg"], k * 2)
                act.activation(pt0_hi[:], ps_0[:], ACT.Copy).then_inc(s["z_hi_made"], 1)

            def elu_exp(k, half):
                n = k * 2 + half
                wait(act, s["elu_relu"], n + 1)
                for g in range(2):
                    src = (ps_0, ps_s)[half][:, g * D:(g + 1) * D]
                    last = act.activation(hn0[:, 2 * half + g], src, ACT.Exp, scale=zrden[:, 2 * half + g:2 * half + g + 1])
                last.then_inc(s["elu_exped"], 1)

            def iteration(i):
                for t, (pre, att, mid, ffn, post) in slots(i):
                    z = i + 2
                    for m in range(MC):
                        if here(ffn[0]):
                            gelu(*ffn, m)
                        if m == 0 and here(mid[0]):
                            h_norm(*mid)
                        if m == 0 and here(att[0]):
                            x_high(*att)
                        if m == 1 and here(mid[0]):
                            ht_affine(*mid, 0)
                        if m == 2 and here(mid[0]):
                            ht_affine(*mid, 1)
                        if m == 2 and here(att[0]):
                            exps(*att)
                        if m == 2 and t == 2 and here(z):
                            z_exps(z)
                        if m == 3 and here(att[0]):
                            p_high(*att)
                        if m == 4 and here(post[0]):
                            y_norm(*post)
                        if m == 3 and t == 0 and here(pre[0]):
                            r_norm(pre[0])
                        if t == 1 and here(z):
                            if m == 1:
                                x0_norm(z)
                            if m == 2:
                                h0_high(z, 0)
                            if m == 3:
                                wh_high(z, 0)
                            if m == 4:
                                h0_high(z, 1)
                            if m == 5:
                                wh_high(z, 1)
                        if t == 2 and here(z):
                            if m == 4:
                                z_high(z)
                            if m == 6:
                                elu_exp(z, 0)
                                elu_exp(z, 1)

            schedule(iteration, act)

        @block.vector
        def _(dve):
            stt, tt, ts = dve.scalar_tensor_tensor, dve.tensor_tensor, dve.tensor_scalar

            dve.wait_ge(s["w0_in"], 16)
            dve.tensor_copy(w0_hi[:], Y[:, 0:DC, :]).then_inc(s["w0_split"], 0 + 1)
            dve.wait_ge(s["w0_split"], 1)
            tt(w0_lo[:], Y[:, 0:DC, :], w0_hi[:].bitcast(F32), ALU.subtract).then_inc(s["w0_split"], 1)
            dve.wait_ge(s["const_in"], 16 * 11)
            tt(bb_row[:], bb_row[:], H[:, 2, 0:L, :], ALU.add)
            for l in range(L):
                staged = X[:, 0:2, :, :].rearrange("p l g d -> p (l g d)")
                hi, lo = (w[:, l].rearrange("p c n -> p (c n)") for w in (w1_hi, w1_lo))
                dve.wait_ge(s["w1_in"], 16 * (l + 1))
                dve.tensor_copy(hi, staged).then_inc(s["hold_vector"], 1)
                dve.wait_ge(s["hold_vector"], l + 1)
                tt(lo, staged, hi.bitcast(F32), ALU.subtract).then_inc(s["w1_split"], 1)
            dve.wait_ge(s["w1_split"], L)
            dve.wait_ge(s["const_made"], 2)
            dve.memset(zden[:], 0.0).then_inc(s["w1_split"], 1)

            def hold(sem_, n):
                wait(dve, sem_, n)
                if isinstance(n, At):
                    dve.sem_inc(s["hold_vector"], 1)

            def moments(name, n, src):
                st, short = stats[name], name + "st_"
                for g in range(G):
                    last = dve.bn_stats(st["six"][:, g], src(g))
                last.then_inc(s[short + "six"], 1)
                hold(s[short + "six"], n + 1)
                for g in range(G):
                    last = dve.bn_aggr(st["mv"][:, g], st["six"][:, g])
                last.then_inc(s[short + "mv"], 1)
                wait(dve, s[short + "mv"], n + 1)
                ts(st["ve"][:], st["mv"][:, :, 1], EPS, None, ALU.add).then_inc(s[short + "ve"], 1)

            def minus_mean(name, n):
                st, short = stats[name], name + "st_"
                wait(dve, s[short + "rstd"], n + 1)
                stt(out=st["nmr"][:], in0=st["mv"][:, :, 0], scalar=-1.0, in1=st["rstd"][:],
                    op0=ALU.mult, op1=ALU.mult).then_inc(s[short + "nmr"], 1)

            def masks(k):
                wait(dve, s["adj_in"], k * 16 + 16)
                ts(mask0[:], adj_sb[:], 0.0, OFF, ALU.is_le, ALU.mult).then_inc(s["mask_made"], 1)
                wait(dve, s["z_turned"], k)
                tt(kept[:], adj_sb[:], ident[:].rearrange("p (o m) -> p o m", o=1).to_broadcast([P, G, P]),
                   ALU.add).then_inc(s["adj_sum"], 1)
                wait(dve, s["adj_sum"], k + 1)
                wait(dve, s["mask_parked"], k * 16)
                ts(mask_out[:], kept[:], 0.0, OFF, ALU.is_le, ALU.mult).then_inc(s["mask_made"], 1)

            def h0_low(k, half):
                n = k * 2 + half
                wait(dve, s["h0_hi_made"], n + 1)
                wait(dve, s["wh_made"], n)
                stt(out=h0_lo[:].rearrange("p c n -> p (c n)"), in0=ps_0[:], scalar=0.0,
                    in1=h0_hi[:].rearrange("p c n -> p (c n)").bitcast(F32),
                    op0=ALU.max, op1=ALU.subtract).then_inc(s["h0_split"], 1)

            def wh_scores(k, half):
                n = k * 2 + half
                wait(dve, s["wh_made"], n + 1)
                for g in range(2):
                    for j in range(2):
                        last = dve.tensor_tensor_reduce(
                            out=junk[:, 2 * g + j], in0=ps_0[:, g * D:(g + 1) * D], in1=a0_row[:, j], scale=1.0, scalar=0.0,
                            op0=ALU.mult, op1=ALU.add, accum_out=e0[:, j, 2 * half + g:2 * half + g + 1])
                last.then_inc(s["e0_made"], 1)

            def wh_low(k, half):
                n = k * 2 + half
                wait(dve, s["wh_hi_made"], n + 1)
                tt(wh_lo[:, 2 * half:2 * half + 2].rearrange("p g d -> p (g d)"), ps_0[:],
                   wh_hi[:, 2 * half:2 * half + 2].rearrange("p g d -> p (g d)").bitcast(F32),
                   ALU.subtract).then_inc(s["wh_split"], 1)

            def z_scores(k):
                hold(s["mask_made"], k * 2 + 1)
                hold(s["e0_turned"], k + 1)
                hold(s["x1_made"], k)
                for g in range(G):
                    last = dve.tensor_tensor_reduce(out=U0[:, g], in0=ps_0[:, g * P:(g + 1) * P], in1=mask0[:, g], scale=1.0,
                                                    scalar=-3e38, op0=ALU.add, op1=ALU.max, accum_out=zmax[:, g:g + 1])
                last.then_inc(s["z_scored"], 1)
                wait(dve, s["z_scored"], k + 1)
                tt(zsum[:], zmax[:], e0[:, 0], ALU.add).then_inc(s["z_summed"], 1)
                wait(dve, s["z_summed"], k + 1)
                stt(out=zmx[:], in0=zsum[:], scalar=SLOPE, in1=zsum[:], op0=ALU.mult, op1=ALU.max).then_inc(s["z_maxed"], 1)
                wait(dve, s["z_maxed"], k + 1)
                tt(zbias_a[:], e0[:, 0], zmx[:], ALU.subtract)
                stt(out=zbias_b[:], in0=e0[:, 0], scalar=SLOPE, in1=zmx[:], op0=ALU.mult,
                    op1=ALU.subtract).then_inc(s["z_biased"], 1)

            def z_probs(k):
                wait(dve, s["z_exped"], k + 1)
                for g in range(G):
                    last = stt(out=U0[:, g], in0=U0[:, g], scalar=1.0, in1=EB0[:, g], op0=ALU.mult, op1=ALU.max,
                               accum_out=zden[:, g:g + 1])
                last.then_inc(s["z_probs"], 1)
                wait(dve, s["z_probs"], k + 1)
                dve.reciprocal(zrden[:], zden[:]).then_inc(s["z_rden_made"], 1)
                for g in range(G):
                    last = dve.max(top[:, 0, g], U0[:, g])
                last.then_inc(s["z_top1"], 1)
                hold(s["z_top1"], k + 1)
                for g in range(G):
                    last = dve.match_replace(kept[:, g], top[:, 0, g], U0[:, g], -1.0)
                last.then_inc(s["z_rest"], 1)
                hold(s["z_rest"], k + 1)
                for g in range(G):
                    last = dve.max(top[:, 1, g], kept[:, g])
                last.then_inc(s["z_top2"], 1)
                wait(dve, s["z_top2"], k + 1)
                for g in range(G):
                    last = stt(out=U0[:, g], in0=U0[:, g], scalar=top[:, 1, g, 7:8], in1=U0[:, g], op0=ALU.is_ge,
                               op1=ALU.mult)
                last.then_inc(s["z_kept"], 1)

            def z_low(k):
                wait(dve, s["z_hi_made"], k + 1)
                wait(dve, s["z_agg"], k * 2)
                tt(pt0_lo[:], ps_0[:], pt0_hi[:].bitcast(F32), ALU.subtract).then_inc(s["z_split"], 1)

            def elu_relu(k, half):
                n = k * 2 + half
                wait(dve, s["z_agg"], n + 1)
                wait(dve, s["z_turned"], k + 1)
                wait(dve, s["z_rden_made"], k + 1)
                dst = (U0, EB0)[half][:].rearrange("p g m -> p (g m)")
                for g in range(2):
                    last = ts(dst[:, g * D:(g + 1) * D], (ps_0, ps_s)[half][:, g * D:(g + 1) * D],
                              zrden[:, 2 * half + g:2 * half + g + 1], 0.0, ALU.mult, ALU.max)
                last.then_inc(s["elu_relu"], 1)

            def elu_sum(k, half):
                n = k * 2 + half
                r = (U0, EB0)[half][:].rearrange("p g m -> p (g m)")
                e = hn0[:, 2 * half:2 * half + 2].rearrange("p g d -> p (g d)")
                wait(dve, s["elu_exped"], n + 1)
                stt(out=r, in0=e, scalar=1.0, in1=r, op0=ALU.min, op1=ALU.add).then_inc(s["elu_sum"], 1)

            def x1_sum(k):
                wait(dve, s["elu_sum"], k * 2 + 2)
                for half in range(2):
                    r = (U0, EB0)[half][:].rearrange("p g m -> p (g m)")
                    xx = x1[:, 2 * half:2 * half + 2].rearrange("p g d -> p (g d)")
                    last = stt(out=xx, in0=r, scalar=-1.0, in1=xx, op0=ALU.add, op1=ALU.add)
                last.then_inc(s["x1_made"], 1)

            def node_scores(k, l):
                n = seq(k, l)
                wait(dve, s_x[l], k + 1)
                for g in range(G):
                    for j in range(2):
                        last = dve.tensor_tensor_reduce(
                            out=junk[:, 2 * g + j], in0=X[:, l, g], in1=wij_row[:, l, j], scale=1.0, scalar=0.0,
                            op0=ALU.mult, op1=ALU.add, accum_out=sij[:, l, j, g:g + 1])
                last.then_inc(s["sij_made"], 1)
                wait(dve, s["sij_made"], n + 1)
                ts(sib[:, l], sij[:, l, 0], b_att[:, l:l + 1], None, ALU.add).then_inc(s["sib_made"], 1)

            def scores(k, l):
                n = seq(k, l)
                hold(s_mask[l], k * 16 + 16)
                hold(s["sj_turned"], n + 1)
                hold(s["p_turned"], n)
                hold(s["sib_made"], n + 1)
                for g in range(G):
                    last = dve.tensor_tensor_reduce(out=U[:, g], in0=ps_s[:, g * P:(g + 1) * P], in1=mask_in[:, l, g], scale=1.0,
                                                    scalar=-3e38, op0=ALU.add, op1=ALU.max, accum_out=smax[:, g:g + 1])
                last.then_inc(s["scored"], 1)
                wait(dve, s["scored"], n + 1)
                tt(ssum[:], smax[:], sib[:, l], ALU.add).then_inc(s["summed"], 1)
                wait(dve, s["summed"], n + 1)
                stt(out=smx[:], in0=ssum[:], scalar=SLOPE, in1=ssum[:], op0=ALU.mult, op1=ALU.max).then_inc(s["maxed"], 1)
                wait(dve, s["maxed"], n + 1)
                tt(bias_a[:], sib[:, l], smx[:], ALU.subtract)
                stt(out=bias_b[:], in0=sib[:, l], scalar=SLOPE, in1=smx[:], op0=ALU.mult,
                    op1=ALU.subtract).then_inc(s["biased"], 1)

            def probs(k, l):
                n = seq(k, l)
                wait(dve, s["exped"], n + 1)
                for g in range(G):
                    last = stt(out=U[:, g], in0=U[:, g], scalar=1.0, in1=EB[:, g], op0=ALU.mult, op1=ALU.max,
                               accum_out=den[:, g:g + 1])
                last.then_inc(s["probs"], 1)
                wait(dve, s["probs"], n + 1)
                dve.reciprocal(rden[:], den[:]).then_inc(s["rden_made"], 1)

            def p_low(k, l):
                n = seq(k, l)
                wait(dve, s["p_hi_made"], n + 1)
                wait(dve, s["agg_made"], n * 2)
                tt(pt_lo[:], ps_s[:], pt_hi[:].bitcast(F32), ALU.subtract).then_inc(s["p_split"], 1)

            def y1_sum(k, l, half):
                n = seq(k, l)
                wait(dve, s["rden_made"], n + 1)
                wait(dve, s["x_lo_made"], n + 1)
                wait(dve, s["agg_made"], n * 2 + half + 1)
                for g in range(2):
                    j = 2 * half + g
                    last = stt(out=X[:, l, j], in0=ps_ag[:, g * D:(g + 1) * D], scalar=rden[:, j:j + 1], in1=X[:, l, j],
                               op0=ALU.mult, op1=ALU.add)
                last.then_inc(s["y1_made"], 1)

            def y1_moments(k, l):
                n = seq(k, l)
                wait(dve, s["y1_made"], n * 2 + 2)
                moments("h", n, lambda g: X[:, l, g])

            def ht_parts(k, l, d):
                n = seq(k, l)
                wait(dve, s["ht_f_made"], n * 2 + d + 1)
                wait(dve, s["mm1_made"], (n - 1) * MC)
                dve.tensor_copy(ht_hi[:, l, d], ht_f[:]).then_inc(s["ht_hi_made"], 1)
                wait(dve, s["ht_hi_made"], n * 2 + d + 1)
                tt(ht_lo[:, l, d], ht_f[:], ht_hi[:, l, d].bitcast(F32), ALU.subtract).then_inc(s["ht_split"], 1)

            def h_bias(k, l):
                n = seq(k, l)
                wait(dve, s["h_scaled"], n + 1)
                tt(H[:, l], H[:, l], bb_row[:, l:l + 1, :].to_broadcast([P, G, D]), ALU.add).then_inc(s["h_res"], 1)

            def y_sum(k, l):
                n = seq(k, l)
                wait(dve, s["h_res"], n + 1)
                wait(dve, s["out_added"], (k - (2 - l)) * 16)
                wait(dve, s["mm2_made"], n * MC + MC)
                for half in range(2):
                    last = tt(Y[:, 2 * half:2 * half + 2].rearrange("p g d -> p (g d)"), ps_ff[half][:],
                              H[:, l, 2 * half:2 * half + 2].rearrange("p g d -> p (g d)"), ALU.add)
                last.then_inc(s["y_made"], 1)
                wait(dve, s["y_made"], n + 1)
                moments("y", n, lambda g: Y[:, g])

            def y_bias(k, l):
                n = seq(k, l)
                wait(dve, s["y_scaled"], n + 1)
                bias = be2_row[:, l:l + 1, :].to_broadcast([P, G, D])
                if l == L - 1:
                    tt(Y[:], Y[:], bias, ALU.add).then_inc(s["y_final"], 1)
                    return
                if not (isinstance(k, int) and k == 0):
                    wait(dve, s["h_turned"], seq(k - 1, l + 1) * 2 + 2)
                    wait(dve, s["h_scaled"], seq(k - 1, l + 1) + 1)
                tt(X[:, l + 1], Y[:], bias, ALU.add).then_inc(s_x[l + 1], 1)

            def iteration(i):
                for t, (pre, att, mid, ffn, post) in slots(i):
                    z = i + 2
                    for m in range(MC):
                        if m == 0:
                            if here(mid[0]):
                                minus_mean("h", seq(*mid))
                            if here(att[0]):
                                scores(*att)
                        if m == 1:
                            if here(mid[0]):
                                ht_parts(*mid, 0)
                        if m == 2:
                            if here(post[0]):
                                y_sum(*post)
                            if here(mid[0]):
                                ht_parts(*mid, 1)
                            if t == 0 and here(pre[0]):
                                wait(dve, s["x1_made"], pre[0] + 1)
                                moments("r", pre[0], lambda g: x1[:, g])
                        if m == 3:
                            if here(att[0]):
                                probs(*att)
                            if t == 0 and here(pre[0]):
                                minus_mean("r", pre[0])
                            if here(post[0]):
                                minus_mean("y", seq(*post))
                            if here(att[0]):
                                p_low(*att)
                        if m == 5:
                            if here(mid[0]):
                                h_bias(*mid)
                            if here(att[0]):
                                y1_sum(*att, 0)
                        if m == 6:
                            if here(post[0]):
                                y_bias(*post)
                            if here(att[0]):
                                y1_sum(*att, 1)
                                y1_moments(*att)
                        if m == 7:
                            if here(pre[0]):
                                node_scores(*pre)
                        if t == 1 and here(z):
                            if m == 0:
                                wait(dve, s["x_in"], z * 16 + 16)
                                moments("x", z, lambda g: x1[:, g])
                                masks(z)
                            if m == 1:
                                minus_mean("x", z)
                            if m == 2:
                                h0_low(z, 0)
                            if m == 3:
                                wh_scores(z, 0)
                                wh_low(z, 0)
                            if m == 4:
                                h0_low(z, 1)
                            if m == 5:
                                wh_scores(z, 1)
                                wh_low(z, 1)
                            if m == 6:
                                z_scores(z)
                        if t == 2 and here(z):
                            if m == 3:
                                z_probs(z)
                            if m == 4:
                                z_low(z)
                            if m == 5:
                                elu_relu(z, 0)
                                elu_relu(z, 1)
                            if m == 7:
                                elu_sum(z, 0)
                                elu_sum(z, 1)
                                x1_sum(z)

            schedule(iteration, dve)

        @block.tensor
        def _(pe):
            pe.wait_ge(s["const_made"], 2)
            pe.wait_ge(s["w0_split"], 2)
            pe.wait_ge(s["w1_split"], L)
            pe.wait_ge(s["w2_in"], 16)

            def mm1(k, l, m):
                c = seq(k, l) * MC + m
                if m == 0:
                    wait(pe, s["ht_split"], seq(k, l) * 2 + 2)
                wait(pe, s["gelu_made"], c - 1)
                for d in range(DC):
                    cols = slice(m * P, (m + 1) * P)
                    pe.matmul(ps_mm[m % 2][:], w1_hi[:, l, d, cols], ht_hi[:, l, d], start=(d == 0), stop=False)
                    pe.matmul(ps_mm[m % 2][:], w1_lo[:, l, d, cols], ht_hi[:, l, d], start=False, stop=False)
                    last = pe.matmul(ps_mm[m % 2][:], w1_hi[:, l, d, cols], ht_lo[:, l, d], start=False, stop=(d == DC - 1))
                last.then_inc(s["mm1_made"], 1)

            def mm2(k, l, m):
                c = seq(k, l) * MC + m
                if m == 0:
                    wait(pe, s["y_made"], seq(k, l))
                wait(pe, s["gelu_made"], c + 1)
                for g in range(G):
                    last = pe.matmul(ps_ff[g // 2][:, g % 2 * D:(g % 2 + 1) * D], A[:, m % 4, g * P:(g + 1) * P], w2_sb[:, l, m],
                                     start=(m == 0 and g % 2 == 0), stop=(m == MC - 1 and g % 2 == 1), skip_group_check=True)
                last.then_inc(s["mm2_made"], 1)

            def turn_sj(k, l, t):
                n = seq(k, l)
                wait(pe, s["sij_made"], n + 1)
                wait(pe, s["p_split"], n)
                if t == 0:
                    z_done = k + 4
                    wait(pe, s["elu_exped"], (z_done if isinstance(z_done, At) else min(z_done, NG)) * 2)
                for g in range(G):
                    last = pe.transpose(ps_s[:, g * P:(g + 1) * P], sij[:, l, 1, g:g + 1].to_broadcast([P, P]), ident[:])
                last.then_inc(s["sj_turned"], 1)

            def turn_p(k, l):
                n = seq(k, l)
                wait(pe, s["probs"], n + 1)
                for g in range(G):
                    last = pe.transpose(ps_s[:, g * P:(g + 1) * P], U[:, g], ident[:])
                last.then_inc(s["p_turned"], 1)

            def three_products(dst, hi, lo, v_hi, v_lo, first, final):
                pe.matmul(dst, hi, v_hi, start=first, stop=False, skip_group_check=True)
                pe.matmul(dst, hi, v_lo, start=False, stop=False, skip_group_check=True)
                return pe.matmul(dst, lo, v_hi, start=False, stop=final, skip_group_check=True)

            def agg(k, l, half):
                n = seq(k, l)
                wait(pe, s["p_split"], n + 1)
                wait(pe, s["x_lo_made"], n + 1)
                wait(pe, s["y1_made"], n * 2 + half)
                for g in range(2):
                    j = 2 * half + g
                    last = three_products(ps_ag[:, g * D:(g + 1) * D], pt_hi[:, j * P:(j + 1) * P], pt_lo[:, j * P:(j + 1) * P],
                                          x_hi[:, j], x_lo[:, j], g == 0, g == 1)
                last.then_inc(s["agg_made"], 1)

            def turn_h(k, l, d):
                n = seq(k, l) * 2 + d
                wait(pe, s["h_norm"], seq(k, l) + 1)
                wait(pe, s["ht_f_made"], n)
                for g in range(G):
                    last = pe.transpose(ps_ht[:, g * P:(g + 1) * P], X[:, l, g, d * P:(d + 1) * P], ident[:])
                last.then_inc(s["h_turned"], 1)

            def turn_h0(k, half):
                n = k * 2 + half
                wait(pe, s["x_norm"], k + 1)
                wait(pe, s["wh_split"], n)
                wait(pe, s["elu_exped"], k * 2)
                for d in range(DC):
                    for g in range(2):
                        last = pe.transpose(ps_0[:, (2 * d + g) * P:(2 * d + g + 1) * P],
                                            hn0[:, 2 * half + g, d * P:(d + 1) * P], ident[:])
                last.then_inc(s["h0_turned"], 1)

            def wh(k, half):
                n = k * 2 + half
                wait(pe, s["h0_split"], n + 1)
                for g in range(2):
                    for d in range(DC):
                        cols = slice(g * P, (g + 1) * P)
                        last = three_products(ps_0[:, g * D:(g + 1) * D], h0_hi[:, d, cols], h0_lo[:, d, cols],
                                              w0_hi[:, d], w0_lo[:, d], g == 0 and d == 0, g == 1 and d == DC - 1)
                last.then_inc(s["wh_made"], 1)

            def turn_e0(k):
                wait(pe, s["wh_split"], k * 2 + 2)
                for g in range(G):
                    last = pe.transpose(ps_0[:, g * P:(g + 1) * P], e0[:, 1, g:g + 1].to_broadcast([P, P]), ident[:])
                last.then_inc(s["e0_turned"], 1)

            def turn_z(k):
                wait(pe, s["z_kept"], k + 1)
                for g in range(G):
                    last = pe.transpose(ps_0[:, g * P:(g + 1) * P], U0[:, g], ident[:])
                last.then_inc(s["z_turned"], 1)

            def z_agg(k, half, n_att):
                wait(pe, s["z_split"], k + 1)
                if half == 1 and n_att is not None:
                    wait(pe, s["p_split"], n_att)
                for g in range(2):
                    j = 2 * half + g
                    last = three_products((ps_0, ps_s)[half][:, g * D:(g + 1) * D], pt0_hi[:, j * P:(j + 1) * P],
                                          pt0_lo[:, j * P:(j + 1) * P], wh_hi[:, j], wh_lo[:, j], g == 0, g == 1)
                last.then_inc(s["z_agg"], 1)

            def iteration(i):
                for t, (pre, att, mid, ffn, post) in slots(i):
                    z = i + 2
                    for m in range(MC):
                        if here(ffn[0]):
                            mm1(*ffn, m)
                        if m == 0 and here(att[0]):
                            turn_sj(*att, t)
                        if m == 1 and here(mid[0]):
                            turn_h(*mid, 0)
                        if t == 1 and here(z):
                            if m == 2:
                                turn_h0(z, 0)
                            if m == 3:
                                wh(z, 0)
                            if m == 4:
                                turn_h0(z, 1)
                            if m == 5:
                                wh(z, 1)
                            if m == 6:
                                turn_e0(z)
                        if m < 2:
                            if here(post[0]):
                                mm2(*post, MC - 2 + m)
                        elif here(ffn[0]):
                            mm2(*ffn, m - 2)
                        if m == 1 and here(mid[0]):
                            turn_h(*mid, 1)
                        if m == 3 and here(att[0]):
                            turn_p(*att)
                        if m == 4 and here(att[0]):
                            agg(*att, 0)
                        if m == 5 and here(att[0]):
                            agg(*att, 1)
                        if t == 2 and here(z):
                            if m == 3:
                                turn_z(z)
                            if m == 4:
                                z_agg(z, 0, None)
                            if m == 5:
                                z_agg(z, 1, seq(*att) + 1 if here(att[0]) else 0)

            schedule(iteration, pe)


_INS = ["x", "adj", "L0_gnn_W", "L0_gnn_a", "L1_gnn_attn_w", "L1_gnn_attn_b", "L1_gnn_W1", "L1_gnn_b1",
        "L1_gnn_W2", "L1_gnn_b2", "L1_gnn_g1", "L1_gnn_beta1", "L1_gnn_g2", "L1_gnn_beta2"]


def kernel(**inputs):
    import numpy as np
    import concourse.bacc as bacc
    from concourse import mybir as mb
    from concourse.bass_utils import run_bass_kernel_spmd

    nc = bacc.Bacc("TRN2", target_bir_lowering=False, num_devices=1, dynamic_dma_scratch_size=4096)
    arrays, args = {}, []
    for name in _INS:
        a = np.ascontiguousarray(inputs[name])
        arrays["in_" + name] = a
        args.append(nc.dram_tensor("in_" + name, a.shape, mb.dt.from_np(a.dtype), kind="ExternalInput").ap())
    args.append(nc.dram_tensor("out_0", (B, P, D), F32, kind="ExternalOutput").ap())
    build_program(nc, *args)
    r = run_bass_kernel_spmd(nc, [arrays], core_ids=[0])
    return r.results[0]["out_0"]
```

```python
from contextlib import ExitStack

import concourse.bass as bass
from concourse import mybir

F32 = mybir.dt.float32
F32R = mybir.dt.float32r
BF16 = mybir.dt.bfloat16
I32 = mybir.dt.int32
ALU = mybir.AluOpType
ACT = mybir.ActivationFunctionType

P = 128
D = 256
G = 4
B = 128
NG = B // G
L = 3
HID = 4 * D
MC = HID // P
DC = D // P
TOPK_ROUNDS = 2
EPS = 1e-5
SLOPE = 0.2
OFF = -2.0 ** 100
FIRST_STEADY, LAST_STEADY = 4, NG - 3
SPLIT = [m for m in range(MC) if m % 2]
WHOLE = [m for m in range(MC) if m % 2 == 0]


class At:

    def __init__(self, i, a, b):
        self.i, self.a, self.b = i, a, b

    def __mod__(self, c):
        assert c == 2 and self.a % 2 == 0
        return self.b % 2

    def __add__(self, c):
        return At(self.i, self.a, self.b + c)

    def __sub__(self, c):
        return self + (-c)

    def __mul__(self, c):
        return At(self.i, self.a * c, self.b * c)

    def value(self):
        return self.i * self.a + self.b


def value(n):
    return n.value() if isinstance(n, At) else n


def here(k):
    return isinstance(k, At) or 0 <= k < NG


def seq(k, l):
    if isinstance(k, At):
        return k * L + ((L + 1) * l - L)
    at = L * k + (L + 1) * l
    return sum(L * kk + (L + 1) * ll < at for kk in range(NG) for ll in range(L))


def before_last(k, l):
    if isinstance(k, At):
        return seq(k, l) - 1
    at = L * k + (L + 1) * l - 1
    return sum(L * kk + (L + 1) * ll < at for kk in range(NG) for ll in range(L))


def some(n):
    return isinstance(n, At) or n > 0


def settle(eng, held, n):
    if isinstance(n, At):
        eng.sem_inc(held, 1)


MM2_LAG = 2


def build_program(nc, x, adj, W0, a0, attn_w, attn_b, W1, b1, W2, b2, g1, be1, g2, be2, out):
    ctx = ExitStack()
    with ctx:
        def sb(name, shape, dt=F32):
            return ctx.enter_context(nc.sbuf_tensor(name, [P] + shape, dt))

        def bank(name):
            return ctx.enter_context(nc.psum_tensor(name, [P, 512], F32))

        def sem(name):
            return ctx.enter_context(nc.semaphore(name))

        w1_hi = sb("w1_hi", [L, DC, HID], F32R)
        w1_lo = sb("w1_lo", [L, DC, HID], F32R)
        w2_f = sb("w2_f", [L, len(WHOLE), D])
        w2_hi = sb("w2_hi", [L, len(SPLIT), D], F32R)
        w2_lo = sb("w2_lo", [L, len(SPLIT), D], F32R)
        w0_hi = sb("w0_hi", [DC, D], F32R)
        w0_lo = sb("w0_lo", [DC, D], F32R)
        a0_row = sb("a0_row", [2, D])
        wij_row = sb("wij_row", [L, 2, D])
        b_att = sb("b_att", [L])
        g1_row = sb("g1_row", [L, D])
        bb_row = sb("bb_row", [L, D])
        g2_row = sb("g2_row", [L, D])
        be2_row = sb("be2_row", [L, D])
        g1_col = sb("g1_col", [L, DC])
        be1_col = sb("be1_col", [L, DC])
        b1_col = sb("b1_col", [L, MC])
        ident = sb("ident", [P])
        minus_half = sb("minus_half", [G])

        X = sb("X", [L, G, D])
        H = sb("H", [2, G, D])
        ht_hi = sb("ht_hi", [2, DC, G * P], F32R)
        ht_lo = sb("ht_lo", [2, DC, G * P], F32R)
        ht_f = sb("ht_f", [G * P])
        Y = sb("Y", [G, D])
        x1 = sb("x1", [G, D])
        adj_sb = sb("adj_sb", [G, P], I32)
        mask0 = sb("mask0", [G, P], BF16)
        mask_out = sb("mask_out", [G, P], BF16)
        mask_in = sb("mask_in", [L, G, P], BF16)
        U = sb("U", [G, P])
        EB = sb("EB", [G, P])
        pt_hi = sb("pt_hi", [G * P], F32R)
        pt_lo = sb("pt_lo", [G * P], F32R)
        x_hi = sb("x_hi", [G, D], F32R)
        x_lo = sb("x_lo", [G, D], F32R)
        A = sb("A", [3, G * P])
        a_hi = sb("a_hi", [2, G * P], F32R)
        a_lo = sb("a_lo", [2, G * P], F32R)
        hn0 = sb("hn0", [G, D])
        h0_hi = sb("h0_hi", [DC, 2 * P], F32R)
        h0_lo = sb("h0_lo", [DC, 2 * P], F32R)
        wh_hi = sb("wh_hi", [G, D], F32R)
        wh_lo = sb("wh_lo", [G, D], F32R)
        UE0 = sb("UE0", [2, G, P])
        U0, EB0 = UE0[:, 0], UE0[:, 1]
        pt0_hi = sb("pt0_hi", [G * P], F32R)
        pt0_lo = sb("pt0_lo", [G * P], F32R)
        junk = sb("junk", [8, D], BF16)

        def stats_of(name):
            return dict(six=sb(name + "_six", [G, 6]), mv=sb(name + "_mv", [G, 2]), ve=sb(name + "_ve", [G]),
                        rstd=sb(name + "_rstd", [G]), nmr=sb(name + "_nmr", [G]))

        stats = {n: stats_of("st_" + n) for n in ("x", "r", "h", "y")}
        sij = sb("sij", [L, 2, G])
        sib = sb("sib", [L, G])
        smax, ssum, smx, bias_a, bias_b, den, rden = (
            sb("a_" + n, [G]) for n in ("smax", "ssum", "smx", "bias_a", "bias_b", "den", "rden"))
        e0 = sb("e0", [2, G])
        zmax, zsum, zmx, zbias_a, zbias_b, zden, zrden = (
            sb("z_" + n, [G]) for n in ("smax", "ssum", "smx", "bias_a", "bias_b", "den", "rden"))
        top = sb("top", [TOPK_ROUNDS, G, 8])
        kept = EB0

        ps_mm = [bank("ps_mm0"), bank("ps_mm1")]
        ps_ff = [bank("ps_ff0"), bank("ps_ff1")]
        ps_s, ps_ag, ps_ht, ps_0 = bank("ps_s"), bank("ps_ag"), bank("ps_ht"), bank("ps_0")

        mask_park = nc.dram_tensor("mask_park", [NG, P, G * P], BF16, kind="Internal").ap()

        s = {}
        for name in (
            "const_in", "w0_in", "w1_in", "w2_in", "w2_staged", "w1_hi_made", "const_made", "ident_zero", "w1_split", "w0_split", "hold_vector", "hold_sync",
            "hold_pool", "x_in", "adj_in", "mask_parked", "mask_made", "adj_sum", "x1_out", "out_added",
            "xst_six", "xst_mv", "xst_ve", "xst_rstd", "xst_nmr", "x_norm",
            "h0_turned", "h0_hi_made", "h0_split", "wh_made", "wh_hi_made", "wh_split", "e0_made",
            "e0_turned", "z_scored", "z_summed", "z_maxed", "z_biased", "z_exped", "z_probs", "z_top1", "z_rest", "z_top2",
            "z_kept", "z_turned", "z_hi_made", "z_split", "z_agg", "z_rden_made", "z_out_made", "elu_exped", "elu_plus", "elu_minus", "x1_made",
            "rst_six", "rst_mv", "rst_ve", "rst_rstd", "rst_nmr",
            "sij_made", "sib_made", "sj_turned", "scored", "summed", "maxed", "biased", "exped", "probs", "p_turned",
            "p_hi_made", "p_split", "x_hi_made", "x_lo_made", "agg_made", "rden_made", "y1_made",
            "hst_six", "hst_mv", "hst_ve", "hst_rstd", "hst_nmr", "h_norm", "h_turned", "ht_f_made", "ht_hi_made", "ht_split",
            "h_scaled", "h_res", "mm1_made", "gelu_made", "a_hi_made", "a_split", "mm2_made",
            "y_made", "yst_six", "yst_mv", "yst_ve", "yst_rstd", "yst_nmr", "y_norm", "y_scaled", "y_final",
        ):
            s[name] = sem(name)
        s_x = [sem(f"x_ready{l}") for l in range(L)]
        s_mask = [sem(f"mask_in{l}") for l in range(L)]

        x_g = x.rearrange("(k g) n d -> k n g d", g=G)
        adj_g = adj.rearrange("(k g) n m -> k n g m", g=G)
        out_g = out.rearrange("(k g) n d -> k n g d", g=G)

        CONSTS = 10
        STAGED = 2
        LOADS0 = 16

        def turn(m):
            return m // 2 % 2 if m in WHOLE else 2

        def row(ap, n):
            return ap.rearrange("(o n) -> o n", o=1).to_broadcast([P, n])

        def schedule(iteration, eng):
            for i in range(-2, FIRST_STEADY):
                iteration(i)
            with eng.Fori(0, (LAST_STEADY + 1 - FIRST_STEADY) // 2) as j:
                iteration(At(j, 2, FIRST_STEADY))
                iteration(At(j, 2, FIRST_STEADY + 1))
            for i in range(LAST_STEADY + 1, NG + L):
                iteration(i)

        def pair(i, t, o):
            l = (t - o) % L
            return i + (t - o - (L + 1) * l) // L, l

        block = ctx.enter_context(nc.Block())

        @block.sync
        def _(sp):
            sp.dma_start(Y[:, 0:DC, :], W0.rearrange("(c p) n -> p c n", p=P)).then_inc(s["w0_in"], 16)
            sp.dma_start(X[:, 0:2, :, :].rearrange("p l g d -> p (l g d)"),
                         W1[0].rearrange("(c p) n -> p c n", p=P)).then_inc(s["w1_in"], 16)
            for t, src in ((a0_row, row(a0.rearrange("n o -> (n o)"), 2 * D)), (wij_row, row(attn_w.rearrange("l n -> (l n)"), L * 2 * D)),
                           (b_att, row(attn_b, L)), (g1_row, row(g1.rearrange("l n -> (l n)"), L * D)),
                           (bb_row, row(be1.rearrange("l n -> (l n)"), L * D)), (g2_row, row(g2.rearrange("l n -> (l n)"), L * D)),
                           (be2_row, row(be2.rearrange("l n -> (l n)"), L * D))):
                shape = "p a b -> p (a b)" if len(t.shape) == 3 else "p a b c -> p (a b c)"
                dst = t[:] if len(t.shape) == 2 else t[:].rearrange(shape)
                sp.dma_start(dst, src).then_inc(s["const_in"], 16)
            with nc.allow_non_contiguous_dma(reason="three short columns, once"):
                sp.dma_start(g1_col[:], g1.rearrange("l (c p) -> p l c", p=P)).then_inc(s["const_in"], 16)
                sp.dma_start(be1_col[:], be1.rearrange("l (c p) -> p l c", p=P)).then_inc(s["const_in"], 16)
                sp.dma_start(b1_col[:], b1.rearrange("l (c p) -> p l c", p=P)).then_inc(s["const_in"], 16)
            sp.dma_start(hn0[:, 0:L, :].rearrange("p g d -> p (g d)"),
                         row(b2.rearrange("l n -> (l n)"), L * D)).then_inc(s["const_in"], 16)
            for l in range(L):
                chunks = W2[l].rearrange("(c two p) n -> p c two n", two=2, p=P)
                staged = (H[:, 0], H[:, 1], X[:, 2])[l]
                sp.dma_start(w2_f[:, l], chunks[:, :, 0]).then_inc(s["w2_in"], 16)
                sp.dma_start(staged, chunks[:, :, 1]).then_inc(s["w2_staged"], 16)

            def load_layers():
                for l in range(1, L):
                    sp.wait_ge(s["w1_split"], 2 * l - 1)
                    sp.dma_start(X[:, 0:2, :, :].rearrange("p l g d -> p (l g d)"),
                                 W1[l].rearrange("(c p) n -> p c n", p=P)).then_inc(s["w1_in"], 16)

            def load_x(k):
                if not here(k):
                    return
                if some(k):
                    sp.wait_ge(s_x[0], value(k))
                settle(sp, s["hold_sync"], k)
                if some(k * 16):
                    sp.wait_ge(s["x1_out"], value(k * 16))
                settle(sp, s["hold_sync"], k * 16)
                sp.dma_start(x1[:], x_g[value(k)]).then_inc(s["x_in"], 16)

            def load_adj(k):
                if not here(k):
                    return
                if some(k * 2):
                    sp.wait_ge(s["mask_made"], value(k * 2))
                settle(sp, s["hold_sync"], k * 2)
                sp.dma_start(adj_sb[:], adj_g[value(k)]).then_inc(s["adj_in"], 16)

            def park_mask(k):
                if not here(k):
                    return
                sp.wait_ge(s["mask_made"], value(k * 2 + 2))
                settle(sp, s["hold_sync"], k * 2 + 2)
                sp.dma_start(mask_park[value(k)], mask_out[:].rearrange("p g m -> p (g m)")).then_inc(s["mask_parked"], 16)

            def store_x1(k):
                if not here(k):
                    return
                sp.wait_ge(s["x1_made"], value(k + 1))
                settle(sp, s["hold_sync"], k + 1)
                sp.dma_start(out_g[value(k)], x1[:]).then_inc(s["x1_out"], 16)

            def load_mask(k, l):
                if not here(k):
                    return
                sp.wait_ge(s["mask_parked"], value(k * 16 + 16))
                settle(sp, s["hold_sync"], k * 16 + 16)
                if not (isinstance(k, int) and k == 0):
                    sp.wait_ge(s["scored"], value(seq(k - 1, l) + 1))
                    settle(sp, s["hold_sync"], seq(k - 1, l) + 1)
                sp.dma_start(mask_in[:, l].rearrange("p g m -> p (g m)"), mask_park[value(k)]).then_inc(s_mask[l], 16)

            def iteration(i):
                load_mask(i + 1, 0)
                load_mask(i, 1)
                load_adj(i + 2)
                store_x1(i + 1)
                load_x(i + 2)
                park_mask(i + 2)
                load_mask(i - 1, 2)
                if isinstance(i, int) and i == -2:
                    load_layers()

            schedule(iteration, sp)
            sp.wait_ge(s["out_added"], 16 * NG)
            sp.wait_ge(s["x1_out"], 16 * NG)

        @block.gpsimd
        def _(pool):
            pool.memset(ident[:], 0.0).then_inc(s["ident_zero"], 1)
            pool.wait_ge(s["ident_zero"], 1)
            pool.affine_select(out=ident[:], in_=ident[:], compare_op=ALU.not_equal, fill=1.0, base=0,
                               pattern=[[-1, P]], channel_multiplier=1).then_inc(s["const_made"], 1)
            pool.memset(minus_half[:], -0.5).then_inc(s["const_made"], 1)
            pool.wait_ge(s["const_made"], 2)

            def rstd(name, k, l=None):
                if not here(k):
                    return
                n = k if l is None else seq(k, l)
                st, short = stats[name], name + "st_"
                pool.wait_ge(s[short + "ve"], value(n + 1))
                pool.tensor_tensor(st["rstd"][:], st["ve"][:], minus_half[:], ALU.pow).then_inc(s[short + "rstd"], 1)

            def x_low(k, l):
                if not here(k):
                    return
                n = seq(k, l)
                pool.wait_ge(s["x_hi_made"], value(n + 1))
                if some(n * 2):
                    pool.wait_ge(s["agg_made"], value(n * 2))
                pool.tensor_tensor(x_lo[:], X[:, l], x_hi[:].bitcast(F32), ALU.subtract).then_inc(s["x_lo_made"], 1)

            def h_scale(k, l):
                if not here(k):
                    return
                n = seq(k, l)
                pool.wait_ge(s["h_norm"], value(n + 1))
                if some(before_last(k, l)):
                    pool.wait_ge(s["y_made"], value(before_last(k, l)))
                pool.tensor_tensor(H[:, k % 2], X[:, l], g1_row[:, l:l + 1, :].to_broadcast([P, G, D]),
                                   ALU.mult).then_inc(s["h_scaled"], 1)

            def h_bias(k, l):
                if not here(k):
                    return
                pool.wait_ge(s["h_scaled"], value(seq(k, l) + 1))
                pool.tensor_tensor(H[:, k % 2], H[:, k % 2], bb_row[:, l:l + 1, :].to_broadcast([P, G, D]),
                                   ALU.add).then_inc(s["h_res"], 1)

            def a_low(k, l, m):
                if not here(k):
                    return
                n = seq(k, l) * len(SPLIT) + SPLIT.index(m)
                pool.wait_ge(s["a_hi_made"], value(n + 1))
                if some(seq(k, l) * MC + m - 3):
                    pool.wait_ge(s["mm2_made"], value(seq(k, l) * MC + m - 3))
                pool.tensor_tensor(a_lo[:, m // 2 % 2], A[:, turn(m)], a_hi[:, m // 2 % 2].bitcast(F32),
                                   ALU.subtract).then_inc(s["a_split"], 1)

            def y_scale(k, l):
                if not here(k):
                    return
                n = seq(k, l)
                pool.wait_ge(s["y_norm"], value(n + 1))
                pool.tensor_tensor(Y[:], Y[:], g2_row[:, l:l + 1, :].to_broadcast([P, G, D]),
                                   ALU.mult).then_inc(s["y_scaled"], 1)

            def add_out(k, l):
                if l < L - 1 or not here(k):
                    return
                pool.wait_ge(s["y_final"], value(k + 1))
                settle(pool, s["hold_pool"], k)
                pool.wait_ge(s["x1_out"], value(k * 16 + 16))
                settle(pool, s["hold_pool"], k)
                pool.dma_start(out_g[value(k)], Y[:], accum_op=ALU.add).then_inc(s["out_added"], 16)

            def iteration(i):
                for t in range(L):
                    ffn = pair(i, t, 0)
                    att = pair(i, t, -2)
                    mid = pair(i, t, -1)
                    post = pair(i, t, 1)
                    for m in range(MC):
                        if m in SPLIT:
                            a_low(*ffn, m)
                        if m == 1:
                            h_scale(*mid)
                        if m == 2:
                            rstd("y", *post)
                            x_low(*att)
                        if m == 3:
                            if t == 0:
                                rstd("r", i + 1)
                            y_scale(*post)
                        if m == 6:
                            add_out(*post)
                            h_bias(*ffn)
                        if m == 7:
                            rstd("h", *att)
                            if t == 0:
                                rstd("x", i + 2)

            schedule(iteration, pool)

        @block.scalar
        def _(act):
            act.wait_ge(s["const_in"], 16 * 11)
            act.wait_ge(s["w0_split"], 3)

            def gelu(k, l, m):
                if not here(k):
                    return
                c = seq(k, l) * MC + m
                act.wait_ge(s["mm1_made"], value(c + 1))
                if m in WHOLE:
                    if some(c - 3):
                        act.wait_ge(s["mm2_made"], value(c - 3))
                else:
                    if some(seq(k, l) * len(SPLIT) + SPLIT.index(m)):
                        act.wait_ge(s["a_split"], value(seq(k, l) * len(SPLIT) + SPLIT.index(m)))
                act.activation(A[:, turn(m)], ps_mm[m % 2][:], ACT.Gelu, bias=b1_col[:, l, m:m + 1]).then_inc(s["gelu_made"], 1)
                if m in SPLIT:
                    act.wait_ge(s["gelu_made"], value(c + 1))
                    if some(c - 3):
                        act.wait_ge(s["mm2_made"], value(c - 3))
                    act.activation(a_hi[:, m // 2 % 2], A[:, turn(m)], ACT.Copy).then_inc(s["a_hi_made"], 1)

            def norm(name, short, n, dst, src, func, done):
                st = stats[name]
                act.wait_ge(s[short + "nmr"], value(n + 1))
                for g in range(G):
                    last = act.activation(dst(g), src(g), func, bias=st["nmr"][:, g:g + 1], scale=st["rstd"][:, g:g + 1])
                last.then_inc(done, 1)

            def y_norm(k, l):
                if not here(k):
                    return
                norm("y", "yst_", seq(k, l), lambda g: Y[:, g], lambda g: Y[:, g], ACT.Identity, s["y_norm"])

            def h_norm(k, l):
                if not here(k):
                    return
                norm("h", "hst_", seq(k, l), lambda g: X[:, l, g], lambda g: X[:, l, g], ACT.Identity, s["h_norm"])

            def r_norm(k):
                if not here(k):
                    return
                if isinstance(k, int) and k == 0:
                    act.wait_ge(s["w1_split"], 2 * L)
                else:
                    act.wait_ge(s["h_turned"], value(seq(k - 1, 0) * 2 + 2))
                    act.wait_ge(s["h_scaled"], value(seq(k - 1, 0) + 1))
                norm("r", "rst_", k, lambda g: X[:, 0, g], lambda g: x1[:, g], ACT.Relu, s_x[0])

            def x0_norm(k):
                if not here(k):
                    return
                if some(k):
                    act.wait_ge(s["x1_made"], value(k))
                norm("x", "xst_", k, lambda g: hn0[:, g], lambda g: x1[:, g], ACT.Identity, s["x_norm"])

            def x_high(k, l):
                if not here(k):
                    return
                n = seq(k, l)
                act.wait_ge(s_x[l], value(k + 1))
                if some(n * 2):
                    act.wait_ge(s["agg_made"], value(n * 2))
                act.activation(x_hi[:], X[:, l], ACT.Copy).then_inc(s["x_hi_made"], 1)

            def exps(k, l):
                if not here(k):
                    return
                n = seq(k, l)
                act.wait_ge(s["biased"], value(n + 1))
                if some(n):
                    act.wait_ge(s["probs"], value(n))
                for g in range(G):
                    act.activation(EB[:, g], U[:, g], ACT.Exp, bias=bias_b[:, g:g + 1], scale=SLOPE)
                for g in range(G):
                    last = act.activation(U[:, g], U[:, g], ACT.Exp, bias=bias_a[:, g:g + 1])
                last.then_inc(s["exped"], 1)

            def p_high(k, l):
                if not here(k):
                    return
                n = seq(k, l)
                act.wait_ge(s["p_turned"], value(n + 1))
                if some(n * 2):
                    act.wait_ge(s["agg_made"], value(n * 2))
                act.activation(pt_hi[:], ps_s[:], ACT.Copy).then_inc(s["p_hi_made"], 1)

            def ht_affine(k, l, d):
                if not here(k):
                    return
                n = seq(k, l) * 2 + d
                act.wait_ge(s["h_turned"], value(n + 1))
                if some(n):
                    act.wait_ge(s["ht_split"], value(n))
                act.activation(ht_f[:], ps_ht[:], ACT.Identity, bias=be1_col[:, l, d:d + 1],
                               scale=g1_col[:, l, d:d + 1]).then_inc(s["ht_f_made"], 1)

            def h0_high(k, half):
                if not here(k):
                    return
                n = k * 2 + half
                act.wait_ge(s["h0_turned"], value(n + 1))
                if some(n):
                    act.wait_ge(s["wh_made"], value(n))
                act.activation(h0_hi[:].rearrange("p c n -> p (c n)"), ps_0[:], ACT.Relu).then_inc(s["h0_hi_made"], 1)

            def wh_high(k, half):
                if not here(k):
                    return
                n = k * 2 + half
                act.wait_ge(s["wh_made"], value(n + 1))
                act.wait_ge(s["e0_made"], value(n + 1))
                if some(k * 2):
                    act.wait_ge(s["z_agg"], value(k * 2))
                act.activation(wh_hi[:, 2 * half:2 * half + 2].rearrange("p g d -> p (g d)"), ps_0[:],
                               ACT.Copy).then_inc(s["wh_hi_made"], 1)

            def z_exps(k):
                if not here(k):
                    return
                act.wait_ge(s["z_biased"], value(k + 1))
                for g in range(G):
                    act.activation(EB0[:, g], U0[:, g], ACT.Exp, bias=zbias_b[:, g:g + 1], scale=SLOPE)
                for g in range(G):
                    last = act.activation(U0[:, g], U0[:, g], ACT.Exp, bias=zbias_a[:, g:g + 1])
                last.then_inc(s["z_exped"], 1)

            def z_high(k):
                if not here(k):
                    return
                act.wait_ge(s["z_turned"], value(k + 1))
                if some(k * 2):
                    act.wait_ge(s["z_agg"], value(k * 2))
                act.activation(pt0_hi[:], ps_0[:], ACT.Copy).then_inc(s["z_hi_made"], 1)

            def elu_exp(k):
                if not here(k):
                    return
                act.wait_ge(s["z_out_made"], value(k * 2 + 2))
                act.activation(UE0[:].rearrange("p a g m -> p (a g m)"), hn0[:].rearrange("p g d -> p (g d)"),
                               ACT.Exp).then_inc(s["elu_exped"], 1)

            def iteration(i):
                for t in range(L):
                    ffn = pair(i, t, 0)
                    att = pair(i, t, -2)
                    mid = pair(i, t, -1)
                    post = pair(i, t, 1)
                    for m in range(MC):
                        gelu(*ffn, m)
                        if m == 0:
                            x_high(*att)
                        if m == 1:
                            if t == 1:
                                x0_norm(i + 2)
                            h_norm(*mid)
                        if m == 2:
                            if t == 0:
                                elu_exp(i + 1)
                            if t == 2:
                                z_exps(i + 2)
                            if t == 1:
                                h0_high(i + 2, 0)
                            exps(*att)
                        if m == 3:
                            if t == 1:
                                wh_high(i + 2, 0)
                            ht_affine(*mid, 0)
                        if m == 4:
                            y_norm(*post)
                            if t == 1:
                                h0_high(i + 2, 1)
                            p_high(*att)
                            if t == 2:
                                z_high(i + 2)
                            ht_affine(*mid, 1)
                        if m == 5:
                            if t == 0:
                                r_norm(i + 1)
                            if t == 1:
                                wh_high(i + 2, 1)

            schedule(iteration, act)

        @block.vector
        def _(dve):
            stt, tt, ts = dve.scalar_tensor_tensor, dve.tensor_tensor, dve.tensor_scalar

            dve.wait_ge(s["w0_in"], 16)
            dve.tensor_copy(w0_hi[:], Y[:, 0:DC, :]).then_inc(s["w0_split"], 1)
            dve.wait_ge(s["w0_split"], 1)
            tt(w0_lo[:], Y[:, 0:DC, :], w0_hi[:].bitcast(F32), ALU.subtract).then_inc(s["w0_split"], 1)
            dve.wait_ge(s["const_in"], 16 * 11)
            tt(bb_row[:], bb_row[:], hn0[:, 0:L, :], ALU.add).then_inc(s["w0_split"], 1)
            dve.wait_ge(s["const_made"], 2)

            def split_layers():
                for l in range(L):
                    staged = X[:, 0:2, :, :].rearrange("p l g d -> p (l g d)")
                    hi, lo = (w[:, l].rearrange("p c n -> p (c n)") for w in (w1_hi, w1_lo))
                    dve.wait_ge(s["w1_in"], 16 * (l + 1))
                    dve.tensor_copy(hi, staged).then_inc(s["w1_hi_made"], 1)
                    dve.wait_ge(s["w1_hi_made"], 2 * l + 1)
                    tt(lo, staged, hi.bitcast(F32), ALU.subtract).then_inc(s["w1_split"], 1)
                    staged = (H[:, 0], H[:, 1], X[:, 2])[l]
                    dve.wait_ge(s["w2_staged"], 16 * L)
                    dve.tensor_copy(w2_hi[:, l], staged).then_inc(s["w1_hi_made"], 1)
                    dve.wait_ge(s["w1_hi_made"], 2 * l + 2)
                    tt(w2_lo[:, l], staged, w2_hi[:, l].bitcast(F32), ALU.subtract).then_inc(s["w1_split"], 1)

            def moments(name, n, src):
                st, short = stats[name], name + "st_"
                for g in range(G):
                    last = dve.bn_stats(st["six"][:, g], src(g))
                last.then_inc(s[short + "six"], 1)
                dve.wait_ge(s[short + "six"], value(n + 1))
                settle(dve, s["hold_vector"], n + 1)
                for g in range(G):
                    last = dve.bn_aggr(st["mv"][:, g], st["six"][:, g])
                last.then_inc(s[short + "mv"], 1)
                dve.wait_ge(s[short + "mv"], value(n + 1))
                ts(st["ve"][:], st["mv"][:, :, 1], EPS, None, ALU.add).then_inc(s[short + "ve"], 1)

            def minus_mean(name, k, l=None):
                if not here(k):
                    return
                n = k if l is None else seq(k, l)
                st, short = stats[name], name + "st_"
                dve.wait_ge(s[short + "rstd"], value(n + 1))
                stt(out=st["nmr"][:], in0=st["mv"][:, :, 0], scalar=-1.0, in1=st["rstd"][:],
                    op0=ALU.mult, op1=ALU.mult).then_inc(s[short + "nmr"], 1)

            def x_moments(k):
                if not here(k):
                    return
                dve.wait_ge(s["x_in"], value(k * 16 + 16))
                moments("x", k, lambda g: x1[:, g])
                masks(k)

            def r_moments(k):
                if not here(k):
                    return
                dve.wait_ge(s["x1_made"], value(k + 1))
                moments("r", k, lambda g: x1[:, g])

            def masks(k):
                dve.wait_ge(s["adj_in"], value(k * 16 + 16))
                ts(mask0[:], adj_sb[:], 0.0, OFF, ALU.is_le, ALU.mult).then_inc(s["mask_made"], 1)
                if some(k):
                    dve.wait_ge(s["x1_made"], value(k))
                tt(kept, adj_sb[:], ident[:].rearrange("p (o m) -> p o m", o=1).to_broadcast([P, G, P]),
                   ALU.add).then_inc(s["adj_sum"], 1)
                dve.wait_ge(s["adj_sum"], value(k + 1))
                if some(k * 16):
                    dve.wait_ge(s["mask_parked"], value(k * 16))
                ts(mask_out[:], kept, 0.0, OFF, ALU.is_le, ALU.mult).then_inc(s["mask_made"], 1)

            def h0_low(k, half):
                if not here(k):
                    return
                n = k * 2 + half
                dve.wait_ge(s["h0_hi_made"], value(n + 1))
                if some(n):
                    dve.wait_ge(s["wh_made"], value(n))
                stt(out=h0_lo[:].rearrange("p c n -> p (c n)"), in0=ps_0[:], scalar=0.0,
                    in1=h0_hi[:].rearrange("p c n -> p (c n)").bitcast(F32),
                    op0=ALU.max, op1=ALU.subtract).then_inc(s["h0_split"], 1)

            def wh_scores(k, half):
                if not here(k):
                    return
                n = k * 2 + half
                dve.wait_ge(s["wh_made"], value(n + 1))
                for g in range(2):
                    for j in range(2):
                        last = dve.tensor_tensor_reduce(
                            out=junk[:, 2 * g + j], in0=ps_0[:, g * D:(g + 1) * D], in1=a0_row[:, j], scale=1.0, scalar=0.0,
                            op0=ALU.mult, op1=ALU.add, accum_out=e0[:, j, 2 * half + g:2 * half + g + 1])
                last.then_inc(s["e0_made"], 1)

            def wh_low(k, half):
                if not here(k):
                    return
                n = k * 2 + half
                dve.wait_ge(s["wh_hi_made"], value(n + 1))
                tt(wh_lo[:, 2 * half:2 * half + 2].rearrange("p g d -> p (g d)"), ps_0[:],
                   wh_hi[:, 2 * half:2 * half + 2].rearrange("p g d -> p (g d)").bitcast(F32),
                   ALU.subtract).then_inc(s["wh_split"], 1)

            def z_scores(k):
                if not here(k):
                    return
                dve.wait_ge(s["mask_made"], value(k * 2 + 1))
                settle(dve, s["hold_vector"], k * 2 + 1)
                dve.wait_ge(s["e0_turned"], value(k + 1))
                settle(dve, s["hold_vector"], k + 1)
                if some(k):
                    dve.wait_ge(s["x1_made"], value(k))
                settle(dve, s["hold_vector"], k)
                for g in range(G):
                    last = dve.tensor_tensor_reduce(out=U0[:, g], in0=ps_0[:, g * P:(g + 1) * P], in1=mask0[:, g], scale=1.0,
                                                    scalar=-3e38, op0=ALU.add, op1=ALU.max, accum_out=zmax[:, g:g + 1])
                last.then_inc(s["z_scored"], 1)
                dve.wait_ge(s["z_scored"], value(k + 1))
                tt(zsum[:], zmax[:], e0[:, 0], ALU.add).then_inc(s["z_summed"], 1)
                dve.wait_ge(s["z_summed"], value(k + 1))
                stt(out=zmx[:], in0=zsum[:], scalar=SLOPE, in1=zsum[:], op0=ALU.mult, op1=ALU.max).then_inc(s["z_maxed"], 1)
                dve.wait_ge(s["z_maxed"], value(k + 1))
                tt(zbias_a[:], e0[:, 0], zmx[:], ALU.subtract)
                stt(out=zbias_b[:], in0=e0[:, 0], scalar=SLOPE, in1=zmx[:], op0=ALU.mult,
                    op1=ALU.subtract).then_inc(s["z_biased"], 1)

            def z_probs(k):
                if not here(k):
                    return
                dve.wait_ge(s["z_exped"], value(k + 1))
                for g in range(G):
                    last = stt(out=U0[:, g], in0=U0[:, g], scalar=1.0, in1=EB0[:, g], op0=ALU.mult, op1=ALU.max,
                               accum_out=zden[:, g:g + 1])
                last.then_inc(s["z_probs"], 1)
                dve.wait_ge(s["z_probs"], value(k + 1))
                dve.reciprocal(zrden[:], zden[:]).then_inc(s["z_rden_made"], 1)

            def z_topk(k):
                if not here(k):
                    return
                dve.wait_ge(s["z_probs"], value(k + 1))
                settle(dve, s["hold_vector"], k + 1)
                for g in range(G):
                    last = dve.max(top[:, 0, g], U0[:, g])
                last.then_inc(s["z_top1"], 1)
                dve.wait_ge(s["z_top1"], value(k + 1))
                settle(dve, s["hold_vector"], k + 1)
                for g in range(G):
                    last = dve.match_replace(kept[:, g], top[:, 0, g], U0[:, g], -1.0)
                last.then_inc(s["z_rest"], 1)
                dve.wait_ge(s["z_rest"], value(k + 1))
                settle(dve, s["hold_vector"], k + 1)
                for g in range(G):
                    last = dve.max(top[:, 1, g], kept[:, g])
                last.then_inc(s["z_top2"], 1)
                dve.wait_ge(s["z_top2"], value(k + 1))
                for g in range(G):
                    last = stt(out=U0[:, g], in0=U0[:, g], scalar=top[:, 1, g, 7:8], in1=U0[:, g], op0=ALU.is_ge,
                               op1=ALU.mult)
                last.then_inc(s["z_kept"], 1)

            def z_low(k):
                if not here(k):
                    return
                dve.wait_ge(s["z_hi_made"], value(k + 1))
                if some(k * 2):
                    dve.wait_ge(s["z_agg"], value(k * 2))
                tt(pt0_lo[:], ps_0[:], pt0_hi[:].bitcast(F32), ALU.subtract).then_inc(s["z_split"], 1)

            def z_out(k, half):
                if not here(k):
                    return
                n = k * 2 + half
                dve.wait_ge(s["z_agg"], value(n + 1))
                for g in range(2):
                    last = ts(hn0[:, 2 * half + g], ps_0[:, g * D:(g + 1) * D], zrden[:, 2 * half + g:2 * half + g + 1], None,
                              ALU.mult)
                last.then_inc(s["z_out_made"], 1)

            def elu_plus(k):
                if not here(k):
                    return
                flat = "p g d -> p (g d)"
                dve.wait_ge(s["z_out_made"], value(k * 2 + 2))
                stt(out=x1[:].rearrange(flat), in0=hn0[:].rearrange(flat), scalar=0.0, in1=x1[:].rearrange(flat),
                    op0=ALU.max, op1=ALU.add).then_inc(s["elu_plus"], 1)

            def elu_minus(k):
                if not here(k):
                    return
                e = UE0[:].rearrange("p a g m -> p (a g m)")
                xx = x1[:].rearrange("p g d -> p (g d)")
                dve.wait_ge(s["elu_exped"], value(k + 1))
                ts(e, e, 1.0, -1.0, ALU.min, ALU.add).then_inc(s["elu_minus"], 1)
                dve.wait_ge(s["elu_minus"], value(k + 1))
                tt(xx, xx, e, ALU.add).then_inc(s["x1_made"], 1)

            def node_scores(k, l):
                if not here(k):
                    return
                n = seq(k, l)
                dve.wait_ge(s_x[l], value(k + 1))
                for g in range(G):
                    for j in range(2):
                        last = dve.tensor_tensor_reduce(
                            out=junk[:, 2 * g + j], in0=X[:, l, g], in1=wij_row[:, l, j], scale=1.0, scalar=0.0,
                            op0=ALU.mult, op1=ALU.add, accum_out=sij[:, l, j, g:g + 1])
                last.then_inc(s["sij_made"], 1)
                dve.wait_ge(s["sij_made"], value(n + 1))
                ts(sib[:, l], sij[:, l, 0], b_att[:, l:l + 1], None, ALU.add).then_inc(s["sib_made"], 1)

            def scores(k, l):
                if not here(k):
                    return
                n = seq(k, l)
                dve.wait_ge(s_mask[l], value(k * 16 + 16))
                settle(dve, s["hold_vector"], k * 16 + 16)
                dve.wait_ge(s["sj_turned"], value(n + 1))
                settle(dve, s["hold_vector"], n + 1)
                if some(n):
                    dve.wait_ge(s["p_turned"], value(n))
                settle(dve, s["hold_vector"], n)
                dve.wait_ge(s["sib_made"], value(n + 1))
                settle(dve, s["hold_vector"], n + 1)
                for g in range(G):
                    last = dve.tensor_tensor_reduce(out=U[:, g], in0=ps_s[:, g * P:(g + 1) * P], in1=mask_in[:, l, g], scale=1.0,
                                                    scalar=-3e38, op0=ALU.add, op1=ALU.max, accum_out=smax[:, g:g + 1])
                last.then_inc(s["scored"], 1)
                dve.wait_ge(s["scored"], value(n + 1))
                tt(ssum[:], smax[:], sib[:, l], ALU.add).then_inc(s["summed"], 1)
                dve.wait_ge(s["summed"], value(n + 1))
                stt(out=smx[:], in0=ssum[:], scalar=SLOPE, in1=ssum[:], op0=ALU.mult, op1=ALU.max).then_inc(s["maxed"], 1)
                dve.wait_ge(s["maxed"], value(n + 1))
                tt(bias_a[:], sib[:, l], smx[:], ALU.subtract)
                stt(out=bias_b[:], in0=sib[:, l], scalar=SLOPE, in1=smx[:], op0=ALU.mult,
                    op1=ALU.subtract).then_inc(s["biased"], 1)

            def probs(k, l):
                if not here(k):
                    return
                n = seq(k, l)
                dve.wait_ge(s["exped"], value(n + 1))
                for g in range(G):
                    last = stt(out=U[:, g], in0=U[:, g], scalar=1.0, in1=EB[:, g], op0=ALU.mult, op1=ALU.max,
                               accum_out=den[:, g:g + 1])
                last.then_inc(s["probs"], 1)
                dve.wait_ge(s["probs"], value(n + 1))
                dve.reciprocal(rden[:], den[:]).then_inc(s["rden_made"], 1)

            def p_low(k, l):
                if not here(k):
                    return
                n = seq(k, l)
                dve.wait_ge(s["p_hi_made"], value(n + 1))
                if some(n * 2):
                    dve.wait_ge(s["agg_made"], value(n * 2))
                tt(pt_lo[:], ps_s[:], pt_hi[:].bitcast(F32), ALU.subtract).then_inc(s["p_split"], 1)

            def y1_sum(k, l, half):
                if not here(k):
                    return
                n = seq(k, l)
                dve.wait_ge(s["rden_made"], value(n + 1))
                dve.wait_ge(s["x_lo_made"], value(n + 1))
                dve.wait_ge(s["agg_made"], value(n * 2 + half + 1))
                for g in range(2):
                    j = 2 * half + g
                    last = stt(out=X[:, l, j], in0=ps_ag[:, g * D:(g + 1) * D], scalar=rden[:, j:j + 1], in1=X[:, l, j],
                               op0=ALU.mult, op1=ALU.add)
                last.then_inc(s["y1_made"], 1)

            def y1_moments(k, l):
                if not here(k):
                    return
                n = seq(k, l)
                dve.wait_ge(s["y1_made"], value(n * 2 + 2))
                moments("h", n, lambda g: X[:, l, g])

            def ht_parts(k, l, d):
                if not here(k):
                    return
                n = seq(k, l)
                dve.wait_ge(s["ht_f_made"], value(n * 2 + d + 1))
                if some(before_last(k, l) * MC):
                    dve.wait_ge(s["mm1_made"], value(before_last(k, l) * MC))
                dve.tensor_copy(ht_hi[:, k % 2, d], ht_f[:]).then_inc(s["ht_hi_made"], 1)
                dve.wait_ge(s["ht_hi_made"], value(n * 2 + d + 1))
                tt(ht_lo[:, k % 2, d], ht_f[:], ht_hi[:, k % 2, d].bitcast(F32), ALU.subtract).then_inc(s["ht_split"], 1)

            def y_sum(k, l):
                if not here(k):
                    return
                n = seq(k, l)
                dve.wait_ge(s["h_res"], value(n + 1))
                if some((k - (2 - l)) * 16):
                    dve.wait_ge(s["out_added"], value((k - (2 - l)) * 16))
                dve.wait_ge(s["mm2_made"], value(n * MC + MC))
                for half in range(2):
                    last = tt(Y[:, 2 * half:2 * half + 2].rearrange("p g d -> p (g d)"), ps_ff[half][:],
                              H[:, k % 2, 2 * half:2 * half + 2].rearrange("p g d -> p (g d)"), ALU.add)
                last.then_inc(s["y_made"], 1)
                dve.wait_ge(s["y_made"], value(n + 1))
                moments("y", n, lambda g: Y[:, g])

            def y_bias(k, l):
                if not here(k):
                    return
                n = seq(k, l)
                dve.wait_ge(s["y_scaled"], value(n + 1))
                bias = be2_row[:, l:l + 1, :].to_broadcast([P, G, D])
                if l == L - 1:
                    tt(Y[:], Y[:], bias, ALU.add).then_inc(s["y_final"], 1)
                    return
                if not (isinstance(k, int) and k == 0):
                    dve.wait_ge(s["h_turned"], value(seq(k - 1, l + 1) * 2 + 2))
                    dve.wait_ge(s["h_scaled"], value(seq(k - 1, l + 1) + 1))
                tt(X[:, l + 1], Y[:], bias, ALU.add).then_inc(s_x[l + 1], 1)

            def iteration(i):
                if isinstance(i, int) and i == -1:
                    split_layers()
                for t in range(L):
                    before = pair(i, t, -3)
                    att = pair(i, t, -2)
                    mid = pair(i, t, -1)
                    post = pair(i, t, 1)
                    for m in range(MC):
                        if m == 0:
                            if t == 1:
                                minus_mean("x", i + 2)
                            minus_mean("h", *mid)
                            if t == 2:
                                z_scores(i + 2)
                            y_sum(*post)
                            if t == 0:
                                elu_plus(i + 1)
                            scores(*att)
                            if t == 0:
                                elu_minus(i + 1)
                        if m == 1:
                            if t == 2:
                                z_probs(i + 2)
                            if t == 1:
                                h0_low(i + 2, 0)
                        if m == 3:
                            minus_mean("y", *post)
                            if t == 1:
                                wh_scores(i + 2, 0)
                        if m == 4:
                            probs(*att)
                            if t == 2:
                                z_topk(i + 2)
                            if t == 1:
                                wh_low(i + 2, 0)
                            if t == 0:
                                r_moments(i + 1)
                            ht_parts(*mid, 0)
                            if t == 1:
                                h0_low(i + 2, 1)
                            if t == 0:
                                minus_mean("r", i + 1)
                        if m == 5:
                            p_low(*att)
                            if t == 2:
                                z_low(i + 2)
                        if m == 6:
                            ht_parts(*mid, 1)
                            y_bias(*post)
                            if t == 1:
                                wh_scores(i + 2, 1)
                            y1_sum(*att, 0)
                            if t == 1:
                                wh_low(i + 2, 1)
                            node_scores(*before)
                            if t == 2:
                                z_out(i + 2, 0)
                        if m == 7:
                            y1_sum(*att, 1)
                            y1_moments(*att)
                            if t == 2:
                                z_out(i + 2, 1)
                            if t == 0:
                                x_moments(i + 2)

            schedule(iteration, dve)

        @block.tensor
        def _(pe):
            pe.wait_ge(s["const_made"], 2)
            pe.wait_ge(s["w0_split"], 2)

            def three_products(dst, hi, lo, v_hi, v_lo, first, final):
                pe.matmul(dst, hi, v_hi, start=first, stop=False, skip_group_check=True)
                pe.matmul(dst, hi, v_lo, start=False, stop=False, skip_group_check=True)
                return pe.matmul(dst, lo, v_hi, start=False, stop=final, skip_group_check=True)

            def mm1(k, l, m):
                if not here(k):
                    return
                c = seq(k, l) * MC + m
                if m == 0:
                    pe.wait_ge(s["ht_split"], value(seq(k, l) * 2 + 2))
                    if isinstance(k, int) and k == 0:
                        pe.wait_ge(s["w1_split"], 2 * L)
                        pe.wait_ge(s["w2_in"], 16 * L)
                if some(c - 1):
                    pe.wait_ge(s["gelu_made"], value(c - 1))
                for d in range(DC):
                    cols = slice(m * P, (m + 1) * P)
                    pe.matmul(ps_mm[m % 2][:], w1_hi[:, l, d, cols], ht_hi[:, k % 2, d], start=(d == 0), stop=False)
                    pe.matmul(ps_mm[m % 2][:], w1_lo[:, l, d, cols], ht_hi[:, k % 2, d], start=False, stop=False)
                    last = pe.matmul(ps_mm[m % 2][:], w1_hi[:, l, d, cols], ht_lo[:, k % 2, d], start=False, stop=(d == DC - 1))
                last.then_inc(s["mm1_made"], 1)

            def mm2(k, l, m):
                if not here(k):
                    return
                c = seq(k, l) * MC + m
                if m == 0:
                    if some(seq(k, l)):
                        pe.wait_ge(s["y_made"], value(seq(k, l)))
                if m in WHOLE:
                    pe.wait_ge(s["gelu_made"], value(c + 1))
                    for g in range(G):
                        last = pe.matmul(ps_ff[g // 2][:, g % 2 * D:(g % 2 + 1) * D], A[:, turn(m), g * P:(g + 1) * P],
                                         w2_f[:, l, m // 2], start=(m == 0 and g % 2 == 0), stop=False, skip_group_check=True)
                else:
                    pe.wait_ge(s["a_split"], value(seq(k, l) * len(SPLIT) + SPLIT.index(m) + 1))
                    for g in range(G):
                        cols = slice(g * P, (g + 1) * P)
                        last = three_products(ps_ff[g // 2][:, g % 2 * D:(g % 2 + 1) * D], a_hi[:, m // 2 % 2, cols],
                                              a_lo[:, m // 2 % 2, cols], w2_hi[:, l, m // 2], w2_lo[:, l, m // 2],
                                              False, m == MC - 1 and g % 2 == 1)
                last.then_inc(s["mm2_made"], 1)

            def turn_sj(k, l):
                if not here(k):
                    return
                n = seq(k, l)
                pe.wait_ge(s["sij_made"], value(n + 1))
                if some(n):
                    pe.wait_ge(s["p_split"], value(n))
                for g in range(G):
                    last = pe.transpose(ps_s[:, g * P:(g + 1) * P], sij[:, l, 1, g:g + 1].to_broadcast([P, P]), ident[:])
                last.then_inc(s["sj_turned"], 1)

            def turn_p(k, l):
                if not here(k):
                    return
                n = seq(k, l)
                pe.wait_ge(s["probs"], value(n + 1))
                for g in range(G):
                    last = pe.transpose(ps_s[:, g * P:(g + 1) * P], U[:, g], ident[:])
                last.then_inc(s["p_turned"], 1)

            def agg(k, l, half):
                if not here(k):
                    return
                n = seq(k, l)
                pe.wait_ge(s["p_split"], value(n + 1))
                pe.wait_ge(s["x_lo_made"], value(n + 1))
                if some(n * 2 + half):
                    pe.wait_ge(s["y1_made"], value(n * 2 + half))
                for g in range(2):
                    j = 2 * half + g
                    last = three_products(ps_ag[:, g * D:(g + 1) * D], pt_hi[:, j * P:(j + 1) * P], pt_lo[:, j * P:(j + 1) * P],
                                          x_hi[:, j], x_lo[:, j], g == 0, g == 1)
                last.then_inc(s["agg_made"], 1)

            def turn_h(k, l, d):
                if not here(k):
                    return
                n = seq(k, l) * 2 + d
                pe.wait_ge(s["h_norm"], value(seq(k, l) + 1))
                if some(n):
                    pe.wait_ge(s["ht_f_made"], value(n))
                for g in range(G):
                    last = pe.transpose(ps_ht[:, g * P:(g + 1) * P], X[:, l, g, d * P:(d + 1) * P], ident[:])
                last.then_inc(s["h_turned"], 1)

            def turn_h0(k, half):
                if not here(k):
                    return
                n = k * 2 + half
                pe.wait_ge(s["x_norm"], value(k + 1))
                if some(n):
                    pe.wait_ge(s["wh_split"], value(n))
                if some(k * 2):
                    pe.wait_ge(s["z_out_made"], value(k * 2))
                for d in range(DC):
                    for g in range(2):
                        last = pe.transpose(ps_0[:, (2 * d + g) * P:(2 * d + g + 1) * P],
                                            hn0[:, 2 * half + g, d * P:(d + 1) * P], ident[:])
                last.then_inc(s["h0_turned"], 1)

            def wh(k, half):
                if not here(k):
                    return
                n = k * 2 + half
                pe.wait_ge(s["h0_split"], value(n + 1))
                for g in range(2):
                    for d in range(DC):
                        cols = slice(g * P, (g + 1) * P)
                        last = three_products(ps_0[:, g * D:(g + 1) * D], h0_hi[:, d, cols], h0_lo[:, d, cols],
                                              w0_hi[:, d], w0_lo[:, d], g == 0 and d == 0, g == 1 and d == DC - 1)
                last.then_inc(s["wh_made"], 1)

            def turn_e0(k):
                if not here(k):
                    return
                pe.wait_ge(s["wh_split"], value(k * 2 + 2))
                for g in range(G):
                    last = pe.transpose(ps_0[:, g * P:(g + 1) * P], e0[:, 1, g:g + 1].to_broadcast([P, P]), ident[:])
                last.then_inc(s["e0_turned"], 1)

            def turn_z(k):
                if not here(k):
                    return
                pe.wait_ge(s["z_kept"], value(k + 1))
                for g in range(G):
                    last = pe.transpose(ps_0[:, g * P:(g + 1) * P], U0[:, g], ident[:])
                last.then_inc(s["z_turned"], 1)

            def z_agg(k, half):
                if not here(k):
                    return
                pe.wait_ge(s["z_split"], value(k + 1))
                if some(k * 2 + half):
                    pe.wait_ge(s["z_out_made"], value(k * 2 + half))
                for g in range(2):
                    j = 2 * half + g
                    last = three_products(ps_0[:, g * D:(g + 1) * D], pt0_hi[:, j * P:(j + 1) * P], pt0_lo[:, j * P:(j + 1) * P],
                                          wh_hi[:, j], wh_lo[:, j], g == 0, g == 1)
                last.then_inc(s["z_agg"], 1)

            def iteration(i):
                for t in range(L):
                    ffn = pair(i, t, 0)
                    att = pair(i, t, -2)
                    mid = pair(i, t, -1)
                    post = pair(i, t, 1)
                    for m in range(MC):
                        mm1(*ffn, m)
                        if m == 1:
                            if t == 2:
                                turn_e0(i + 2)
                        if m == 2:
                            turn_sj(*att)
                        if m == 3:
                            turn_h(*mid, 0)
                        if m == 5:
                            turn_h(*mid, 1)
                            if t == 1:
                                turn_h0(i + 2, 1)
                        if m == 6:
                            if t == 1:
                                wh(i + 2, 1)
                        if m == 7:
                            if t == 2:
                                z_agg(i + 2, 0)
                        if m < MM2_LAG:
                            mm2(*post, MC - MM2_LAG + m)
                        else:
                            mm2(*ffn, m - MM2_LAG)
                        if m == 0:
                            if t == 0:
                                z_agg(i + 1, 1)
                        if m == 2:
                            if t == 1:
                                turn_h0(i + 2, 0)
                        if m == 3:
                            if t == 1:
                                wh(i + 2, 0)
                        if m == 4:
                            turn_p(*att)
                        if m == 5:
                            if t == 2:
                                turn_z(i + 2)
                        if m == 6:
                            agg(*att, 0)
                        if m == 7:
                            agg(*att, 1)

            schedule(iteration, pe)


_INS = ["x", "adj", "L0_gnn_W", "L0_gnn_a", "L1_gnn_attn_w", "L1_gnn_attn_b", "L1_gnn_W1", "L1_gnn_b1",
        "L1_gnn_W2", "L1_gnn_b2", "L1_gnn_g1", "L1_gnn_beta1", "L1_gnn_g2", "L1_gnn_beta2"]


def kernel(**inputs):
    import numpy as np
    import concourse.bacc as bacc
    from concourse import mybir as mb
    from concourse.bass_utils import run_bass_kernel_spmd

    nc = bacc.Bacc("TRN2", target_bir_lowering=False, num_devices=1, dynamic_dma_scratch_size=2048)
    arrays, args = {}, []
    for name in _INS:
        a = np.ascontiguousarray(inputs[name])
        arrays["in_" + name] = a
        args.append(nc.dram_tensor("in_" + name, a.shape, mb.dt.from_np(a.dtype), kind="ExternalInput").ap())
    args.append(nc.dram_tensor("out_0", (B, P, D), F32, kind="ExternalOutput").ap())
    build_program(nc, *args)
    r = run_bass_kernel_spmd(nc, [arrays], core_ids=[0])
    return r.results[0]["out_0"]
```

```python
from contextlib import ExitStack

import concourse.bass as bass
from concourse import mybir

F32 = mybir.dt.float32
F32R = mybir.dt.float32r
BF16 = mybir.dt.bfloat16
I32 = mybir.dt.int32
ALU = mybir.AluOpType
ACT = mybir.ActivationFunctionType

P = 128
D = 256
G = 4
B = 128
NG = B // G
L = 3
HID = 4 * D
MC = HID // P
DC = D // P
TOPK_ROUNDS = 2
EPS = 1e-5
SLOPE = 0.2
OFF = -2.0 ** 100
FIRST_STEADY, LAST_STEADY = 4, NG - 3


class At:

    def __init__(self, i, a, b):
        self.i, self.a, self.b = i, a, b

    def __mod__(self, c):
        assert c == 2 and self.a % 2 == 0
        return self.b % 2

    def __add__(self, c):
        return At(self.i, self.a, self.b + c)

    def __sub__(self, c):
        return self + (-c)

    def __mul__(self, c):
        return At(self.i, self.a * c, self.b * c)

    def value(self):
        return self.i * self.a + self.b


def peeled(i, n):
    return isinstance(i, int) and i == n


def value(n):
    return n.value() if isinstance(n, At) else n


def here(k):
    return isinstance(k, At) or 0 <= k < NG


def seq(k, l):
    if isinstance(k, At):
        return k * L + ((L + 1) * l - L)
    at = L * k + (L + 1) * l
    return sum(L * kk + (L + 1) * ll < at for kk in range(NG) for ll in range(L))


def before_last(k, l):
    if isinstance(k, At):
        return seq(k, l) - 1
    at = L * k + (L + 1) * l - 1
    return sum(L * kk + (L + 1) * ll < at for kk in range(NG) for ll in range(L))


def some(n):
    return isinstance(n, At) or n > 0


def settle(eng, held, n):
    if isinstance(n, At):
        eng.sem_inc(held, 1)


MM2_LAG = 2


def build_program(nc, x, adj, W0, a0, attn_w, attn_b, W1, b1, W2, b2, g1, be1, g2, be2, out):
    ctx = ExitStack()
    with ctx:
        def sb(name, shape, dt=F32):
            return ctx.enter_context(nc.sbuf_tensor(name, [P] + shape, dt))

        def bank(name):
            return ctx.enter_context(nc.psum_tensor(name, [P, 512], F32))

        def sem(name):
            return ctx.enter_context(nc.semaphore(name))

        w1_hi = sb("w1_hi", [L, DC, HID], F32R)
        w1_lo = sb("w1_lo", [L, DC, HID], F32R)
        w2_hi = sb("w2_hi", [L, MC, D], F32R)
        w2_lo = sb("w2_lo", [L, MC, D], F32R)
        w0_hi = sb("w0_hi", [DC, D], F32R)
        w0_lo = sb("w0_lo", [DC, D], F32R)
        a0_row = sb("a0_row", [2, D])
        wij_row = sb("wij_row", [L, 2, D])
        b_att = sb("b_att", [L])
        g1_row = sb("g1_row", [L, D])
        bb_row = sb("bb_row", [L, D])
        g2_row = sb("g2_row", [L, D])
        be2_row = sb("be2_row", [L, D])
        g1_col = sb("g1_col", [L, DC])
        be1_col = sb("be1_col", [L, DC])
        b1_col = sb("b1_col", [L, MC])
        ident = sb("ident", [P])
        minus_half = sb("minus_half", [G])

        X = sb("X", [L, G, D])
        H = sb("H", [2, G, D])
        ht_hi = sb("ht_hi", [2, DC, G * P], F32R)
        ht_lo = sb("ht_lo", [2, DC, G * P], F32R)
        x1 = sb("x1", [G, D])
        adj_sb = sb("adj_sb", [G, P], I32)
        mask0 = sb("mask0", [G, P], BF16)
        mask_out = sb("mask_out", [G, P], BF16)
        mask_in = sb("mask_in", [L, G, P], BF16)
        U = sb("U", [G, P])
        EB = sb("EB", [G, P])
        pt_hi = sb("pt_hi", [G * P], F32R)
        pt_lo = sb("pt_lo", [G * P], F32R)
        x_hi = sb("x_hi", [G, D], F32R)
        x_lo = sb("x_lo", [G, D], F32R)
        A = sb("A", [2, G * P])
        a_hi = sb("a_hi", [2, G * P], F32R)
        a_lo = sb("a_lo", [2, G * P], F32R)
        hn0 = sb("hn0", [G, D])
        h0_hi = sb("h0_hi", [DC, 2 * P], F32R)
        h0_lo = sb("h0_lo", [DC, 2 * P], F32R)
        wh_hi = sb("wh_hi", [G, D], F32R)
        wh_lo = sb("wh_lo", [G, D], F32R)
        UE0 = sb("UE0", [2, G, P])
        U0, EB0 = UE0[:, 0], UE0[:, 1]
        pt0_hi = sb("pt0_hi", [G * P], F32R)
        pt0_lo = sb("pt0_lo", [G * P], F32R)
        junk = [t_[:, g].bitcast(BF16) for t_ in (U, EB) for g in range(G)]
        junk0 = [UE0[:, 0, g].bitcast(BF16) for g in range(G)]

        def stats_of(name):
            return dict(six=sb(name + "_six", [G, 6]), mv=sb(name + "_mv", [G, 2]), ve=sb(name + "_ve", [G]),
                        rstd=sb(name + "_rstd", [G]), nmr=sb(name + "_nmr", [G]))

        stats = {n: stats_of("st_" + n) for n in ("x", "r", "h", "y")}
        sij = sb("sij", [L, 2, G])
        sib = sb("sib", [L, G])
        smax, ssum, smx, bias_a, bias_b, den, rden = (
            sb("a_" + n, [G]) for n in ("smax", "ssum", "smx", "bias_a", "bias_b", "den", "rden"))
        e0 = sb("e0", [2, G])
        zmax, zsum, zmx, zbias_a, zbias_b, zden, zrden = (
            sb("z_" + n, [G]) for n in ("smax", "ssum", "smx", "bias_a", "bias_b", "den", "rden"))
        top = sb("top", [TOPK_ROUNDS, G, 8])
        kept = EB0

        ps_mm = [bank("ps_mm0"), bank("ps_mm1")]
        ps_ff = [bank("ps_ff0"), bank("ps_ff1")]
        ps_s, ps_ag, ps_ht, ps_0 = bank("ps_s"), bank("ps_ag"), bank("ps_ht"), bank("ps_0")

        mask_park = nc.dram_tensor("mask_park", [NG, P, G * P], BF16, kind="Internal").ap()

        s = {}
        for name in (
            "const_in", "w0_in", "w1_hi_made", "w2_hi_made", "w2_split", "bb_made", "w1_biased", "b1_made",
            "const_made", "ident_zero", "w1_split", "w0_split", "hold_vector", "hold_sync",
            "hold_pool", "x_in", "adj_in", "mask_parked", "mask_made", "adj_sum", "x1_out", "out_added",
            "xst_six", "xst_mv", "xst_ve", "xst_rstd", "xst_nmr", "x_norm",
            "h0_turned", "h0_hi_made", "h0_split", "wh_made", "wh_hi_made", "wh_split", "e0_made",
            "e0_turned", "z_scored", "z_summed", "z_maxed", "z_biased", "z_exped", "z_probs", "z_top1", "z_rest", "z_top2",
            "z_kept", "z_turned", "z_hi_made", "z_split", "z_agg", "z_rden_made",
            "z_out_made", "elu_exped", "elu_plus", "elu_minus", "x1_made",
            "rst_six", "rst_mv", "rst_ve", "rst_rstd", "rst_nmr",
            "sij_made", "sib_made", "sj_turned", "scored", "summed", "maxed", "biased", "exped", "probs", "p_turned",
            "p_hi_made", "p_split", "x_hi_made", "x_lo_made", "agg_made", "rden_made", "y1_made",
            "hst_six", "hst_mv", "hst_ve", "hst_rstd", "hst_nmr", "h_norm", "h_turned", "ht_hi_made", "ht_split",
            "h_scaled", "h_res", "mm1_made", "gelu_made", "a_hi_made", "a_split", "mm2_made",
            "y_made", "yst_six", "yst_mv", "yst_ve", "yst_rstd", "yst_nmr", "y_norm", "y_scaled", "y_final",
        ):
            s[name] = sem(name)
        s_x = [sem(f"x_ready{l}") for l in range(L)]
        s_w1 = [sem(f"w1_in{l}") for l in range(L)]
        s_w2 = [sem(f"w2_in{l}") for l in range(L)]
        s_mask = [sem(f"mask_in{l}") for l in range(L)]

        x_g = x.rearrange("(k g) n d -> k n g d", g=G)
        adj_g = adj.rearrange("(k g) n m -> k n g m", g=G)
        out_g = out.rearrange("(k g) n d -> k n g d", g=G)

        CONSTS = 11

        w0_stage = U[:].rearrange("p g m -> p (g m)").rearrange("p (c n) -> p c n", c=DC)
        w1_stage = X[:, 1:3].rearrange("p l g d -> p (l g d)").rearrange("p (c n) -> p c n", c=DC)
        w2_stage = H[:].rearrange("p a g d -> p (a g) d")
        b2_row = A[:].rearrange("p a n -> p (a n)")[:, 0:L * D]

        def row(ap, n):
            return ap.rearrange("(o n) -> o n", o=1).to_broadcast([P, n])

        def schedule(iteration, eng):
            for i in range(-2, FIRST_STEADY):
                iteration(i)
            with eng.Fori(0, (LAST_STEADY + 1 - FIRST_STEADY) // 2) as j:
                iteration(At(j, 2, FIRST_STEADY))
                iteration(At(j, 2, FIRST_STEADY + 1))
            for i in range(LAST_STEADY + 1, NG + L):
                iteration(i)

        def pair(i, t, o):
            l = (t - o) % L
            return i + (t - o - (L + 1) * l) // L, l

        block = ctx.enter_context(nc.Block())

        @block.sync
        def _(sp):
            def load_w1(l):
                sp.dma_start(w1_stage, W1[l].rearrange("(c p) n -> p c n", p=P)).then_inc(s_w1[l], 16)

            def load_w2(l):
                sp.dma_start(w2_stage, W2[l].rearrange("(c p) n -> p c n", p=P)).then_inc(s_w2[l], 16)

            sp.dma_start(x1[:], x_g[0]).then_inc(s["x_in"], 16)
            sp.dma_start(w0_stage, W0.rearrange("(c p) n -> p c n", p=P)).then_inc(s["w0_in"], 16)
            sp.dma_start(adj_sb[:], adj_g[0]).then_inc(s["adj_in"], 16)
            for t, src in ((a0_row, row(a0.rearrange("n o -> (n o)"), 2 * D)), (wij_row, row(attn_w.rearrange("l n -> (l n)"), L * 2 * D)),
                           (b_att, row(attn_b, L)), (g1_row, row(g1.rearrange("l n -> (l n)"), L * D)),
                           (bb_row, row(be1.rearrange("l n -> (l n)"), L * D)), (g2_row, row(g2.rearrange("l n -> (l n)"), L * D)),
                           (be2_row, row(be2.rearrange("l n -> (l n)"), L * D))):
                shape = "p a b -> p (a b)" if len(t.shape) == 3 else "p a b c -> p (a b c)"
                dst = t[:] if len(t.shape) == 2 else t[:].rearrange(shape)
                sp.dma_start(dst, src).then_inc(s["const_in"], 16)
            with nc.allow_non_contiguous_dma(reason="three short columns, once"):
                sp.dma_start(g1_col[:], g1.rearrange("l (c p) -> p l c", p=P)).then_inc(s["const_in"], 16)
                sp.dma_start(be1_col[:], be1.rearrange("l (c p) -> p l c", p=P)).then_inc(s["const_in"], 16)
                sp.dma_start(b1_col[:], b1.rearrange("l (c p) -> p l c", p=P)).then_inc(s["const_in"], 16)
            sp.dma_start(b2_row, row(b2.rearrange("l n -> (l n)"), L * D)).then_inc(s["const_in"], 16)
            load_w1(0)
            load_w2(0)

            def load_layers():
                for l in range(1, L):
                    sp.wait_ge(s["w1_split"], l)
                    load_w1(l)
                    sp.wait_ge(s["w2_split"], l)
                    load_w2(l)

            def load_x(k):
                if not here(k):
                    return
                if some(k):
                    sp.wait_ge(s_x[0], value(k))
                settle(sp, s["hold_sync"], k)
                if some(k * 16):
                    sp.wait_ge(s["x1_out"], value(k * 16))
                settle(sp, s["hold_sync"], k * 16)
                sp.dma_start(x1[:], x_g[value(k)]).then_inc(s["x_in"], 16)

            def load_adj(k):
                if not here(k):
                    return
                if some(k * 2):
                    sp.wait_ge(s["mask_made"], value(k * 2))
                settle(sp, s["hold_sync"], k * 2)
                sp.dma_start(adj_sb[:], adj_g[value(k)]).then_inc(s["adj_in"], 16)

            def park_mask(k):
                if not here(k):
                    return
                sp.wait_ge(s["mask_made"], value(k * 2 + 2))
                settle(sp, s["hold_sync"], k * 2 + 2)
                sp.dma_start(mask_park[value(k)], mask_out[:].rearrange("p g m -> p (g m)")).then_inc(s["mask_parked"], 16)

            def store_x1(k):
                if not here(k):
                    return
                sp.wait_ge(s["x1_made"], value(k + 1))
                settle(sp, s["hold_sync"], k + 1)
                sp.dma_start(out_g[value(k)], x1[:]).then_inc(s["x1_out"], 16)

            def load_mask(k, l):
                if not here(k):
                    return
                sp.wait_ge(s["mask_parked"], value(k * 16 + 16))
                settle(sp, s["hold_sync"], k * 16 + 16)
                if not peeled(k, 0):
                    sp.wait_ge(s["scored"], value(seq(k - 1, l) + 1))
                    settle(sp, s["hold_sync"], seq(k - 1, l) + 1)
                sp.dma_start(mask_in[:, l].rearrange("p g m -> p (g m)"), mask_park[value(k)]).then_inc(s_mask[l], 16)

            def iteration(i):
                load_mask(i + 1, 0)
                load_mask(i, 1)
                if not peeled(i, -2):
                    load_adj(i + 2)
                store_x1(i + 1)
                if not peeled(i, -2):
                    load_x(i + 2)
                park_mask(i + 2)
                load_mask(i - 1, 2)
                if isinstance(i, int) and i == -2:
                    load_layers()

            schedule(iteration, sp)
            sp.wait_ge(s["out_added"], 16 * NG)
            sp.wait_ge(s["x1_out"], 16 * NG)

        @block.gpsimd
        def _(pool):
            pool.memset(ident[:], 0.0).then_inc(s["ident_zero"], 1)
            pool.wait_ge(s["ident_zero"], 1)
            pool.affine_select(out=ident[:], in_=ident[:], compare_op=ALU.not_equal, fill=1.0, base=0,
                               pattern=[[-1, P]], channel_multiplier=1).then_inc(s["const_made"], 1)
            pool.memset(minus_half[:], -0.5).then_inc(s["const_made"], 1)
            pool.wait_ge(s["const_made"], 2)

            def rstd(name, k, l=None):
                if not here(k):
                    return
                n = k if l is None else seq(k, l)
                st, short = stats[name], name + "st_"
                pool.wait_ge(s[short + "ve"], value(n + 1))
                pool.tensor_tensor(st["rstd"][:], st["ve"][:], minus_half[:], ALU.pow).then_inc(s[short + "rstd"], 1)


            def x_low(k, l, half):
                if not here(k):
                    return
                n = seq(k, l)
                two = slice(2 * half, 2 * half + 2)
                pool.wait_ge(s["x_hi_made"], value(n + 1))
                if some(n * 2):
                    pool.wait_ge(s["agg_made"], value(n * 2))
                pool.tensor_tensor(x_lo[:, two], X[:, l, two], x_hi[:, two].bitcast(F32),
                                   ALU.subtract).then_inc(s["x_lo_made"], 1)

            def h_scale(k, l, half):
                if not here(k):
                    return
                two = slice(2 * half, 2 * half + 2)
                pool.wait_ge(s["h_norm"], value(seq(k, l) + 1))
                if isinstance(k, int) and seq(k, l) == 0:
                    pool.wait_ge(s["w2_split"], L)
                if l == 0 and some(k - 1):
                    pool.wait_ge(s_x[2], value(k - 1))
                if l == 1 and some(k - 1):
                    pool.wait_ge(s["out_added"], value((k - 1) * 16))
                if l == 2:
                    pool.wait_ge(s_x[1], value(k + 3) if isinstance(k, At) else min(k + 3, NG))
                pool.tensor_tensor(H[:, k % 2, two], X[:, l, two], g1_row[:, l:l + 1, :].to_broadcast([P, 2, D]),
                                   ALU.mult).then_inc(s["h_scaled"], 1)

            def h_bias(k, l, half):
                if not here(k):
                    return
                n = seq(k, l) * 2 + half
                two = slice(2 * half, 2 * half + 2)
                if isinstance(k, int) and n == 0:
                    pool.wait_ge(s["bb_made"], 1)
                pool.wait_ge(s["h_scaled"], value(n + 1))
                pool.tensor_tensor(H[:, k % 2, two], H[:, k % 2, two], bb_row[:, l:l + 1, :].to_broadcast([P, 2, D]),
                                   ALU.add).then_inc(s["h_res"], 1)

            def y_scale(k, l, half):
                if not here(k):
                    return
                two = slice(2 * half, 2 * half + 2)
                pool.wait_ge(s["y_norm"], value(seq(k, l) + 1))
                pool.tensor_tensor(H[:, k % 2, two], H[:, k % 2, two], g2_row[:, l:l + 1, :].to_broadcast([P, 2, D]),
                                   ALU.mult).then_inc(s["y_scaled"], 1)

            def w2_low(l):
                pool.wait_ge(s["w2_hi_made"], l + 1)
                pool.tensor_tensor(w2_lo[:, l], w2_stage, w2_hi[:, l].bitcast(F32),
                                   ALU.subtract).then_inc(s["w2_split"], 1)

            def a_low(k, l, m):
                if not here(k):
                    return
                c = seq(k, l) * MC + m
                pool.wait_ge(s["a_hi_made"], value(c + 1))
                if some(c - 1):
                    pool.wait_ge(s["mm2_made"], value(c - 1))
                pool.tensor_tensor(a_lo[:, m % 2], A[:, m % 2], a_hi[:, m % 2].bitcast(F32),
                                   ALU.subtract).then_inc(s["a_split"], 1)

            def add_out(k, l):
                if l < L - 1 or not here(k):
                    return
                pool.wait_ge(s["y_final"], value(k + 1))
                settle(pool, s["hold_pool"], k)
                pool.wait_ge(s["x1_out"], value(k * 16 + 16))
                settle(pool, s["hold_pool"], k)
                pool.dma_start(out_g[value(k)], H[:, k % 2], accum_op=ALU.add).then_inc(s["out_added"], 16)

            def iteration(i):
                for t in range(L):
                    ffn = pair(i, t, 0)
                    att = pair(i, t, -2)
                    mid = pair(i, t, -1)
                    post = pair(i, t, 1)
                    done = pair(i, t, 2)
                    for m in range(MC):
                        a_low(*ffn, m)
                        if m == 0:
                            if t == 0:
                                h_scale(*ffn, 0)
                                x_low(*att, 0)
                            if t == 1:
                                rstd("h", *mid)
                            if t == 2:
                                h_scale(*ffn, 1)
                        if m == 1:
                            if t == 0:
                                x_low(*att, 1)
                                add_out(*done)
                                rstd("y", *post)
                            if t == 1:
                                x_low(*att, 0)
                                x_low(*att, 1)
                                add_out(*done)
                            if t == 2:
                                x_low(*att, 0)
                                add_out(*done)
                        if m == 2:
                            if t == 0:
                                h_scale(*ffn, 1)
                            if t == 2:
                                rstd("y", *post)
                                x_low(*att, 1)
                        if m == 3:
                            if t == 0:
                                rstd("r", i + 1)
                            if t == 1:
                                rstd("y", *post)
                                h_scale(*ffn, 0)
                        if m == 4:
                            if t == 0:
                                h_bias(*ffn, 0)
                                y_scale(*post, 0)
                            if t == 1:
                                h_scale(*ffn, 1)
                                y_scale(*post, 0)
                            if t == 2:
                                y_scale(*post, 0)
                                y_scale(*post, 1)
                        if m == 5:
                            if t == 0:
                                y_scale(*post, 1)
                            if t == 1:
                                y_scale(*post, 1)
                                rstd("h", *att)
                        if m == 6:
                            if t == 1:
                                h_scale(*mid, 0)
                            if t == 2:
                                h_bias(*ffn, 0)
                                rstd("h", *att)
                        if m == 7:
                            if t == 0:
                                rstd("x", i + 2)
                                if peeled(i, -2):
                                    w2_low(0)
                                    w2_low(1)
                            if t == 1:
                                h_bias(*ffn, 0)
                            if t == 2:
                                if peeled(i, -1):
                                    w2_low(2)
                            h_bias(*ffn, 1)

            schedule(iteration, pool)

        @block.scalar
        def _(act):
            def w1_high(l):
                act.wait_ge(s_w1[l], 16)
                if l == 0:
                    act.wait_ge(s["const_in"], 16 * CONSTS)
                for d in range(DC):
                    last = act.activation(w1_hi[:, l, d], w1_stage[:, d], ACT.Identity, scale=g1_col[:, l, d:d + 1])
                last.then_inc(s["w1_hi_made"], 1)

            def w2_high(l):
                act.wait_ge(s_w2[l], 16)
                act.activation(w2_hi[:, l], w2_stage, ACT.Copy).then_inc(s["w2_hi_made"], 1)

            def gelu(k, l, m):
                if not here(k):
                    return
                c = seq(k, l) * MC + m
                if isinstance(k, int) and seq(k, l) == 0 and m == 0:
                    act.wait_ge(s["b1_made"], 1)
                    act.wait_ge(s["bb_made"], 1)
                act.wait_ge(s["mm1_made"], value(c + 1))
                if some(c - 1):
                    act.wait_ge(s["a_split"], value(c - 1))
                act.activation(A[:, m % 2], ps_mm[m % 2][:], ACT.Gelu, bias=b1_col[:, l, m:m + 1]).then_inc(s["gelu_made"], 1)

            def a_high(k, l, m):
                if not here(k):
                    return
                c = seq(k, l) * MC + m
                act.wait_ge(s["gelu_made"], value(c + 1))
                if some(c - 1):
                    act.wait_ge(s["mm2_made"], value(c - 1))
                act.activation(a_hi[:, m % 2], A[:, m % 2], ACT.Copy).then_inc(s["a_hi_made"], 1)

            def norm(name, short, n, dst, src, func, done):
                st = stats[name]
                act.wait_ge(s[short + "nmr"], value(n + 1))
                for g in range(G):
                    last = act.activation(dst(g), src(g), func, bias=st["nmr"][:, g:g + 1], scale=st["rstd"][:, g:g + 1])
                last.then_inc(done, 1)

            def y_norm(k, l):
                if not here(k):
                    return
                norm("y", "yst_", seq(k, l), lambda g: H[:, k % 2, g], lambda g: H[:, k % 2, g], ACT.Identity, s["y_norm"])

            def h_norm(k, l):
                if not here(k):
                    return
                norm("h", "hst_", seq(k, l), lambda g: X[:, l, g], lambda g: X[:, l, g], ACT.Identity, s["h_norm"])

            def r_norm(k):
                if not here(k):
                    return
                if not peeled(k, 0):
                    act.wait_ge(s["h_turned"], value(seq(k - 1, 0) * 2 + 2))
                    act.wait_ge(s["h_scaled"], value(seq(k - 1, 0) * 2 + 2))
                norm("r", "rst_", k, lambda g: X[:, 0, g], lambda g: x1[:, g], ACT.Relu, s_x[0])

            def x0_norm(k):
                if not here(k):
                    return
                if some(k):
                    act.wait_ge(s["x1_made"], value(k))
                norm("x", "xst_", k, lambda g: hn0[:, g], lambda g: x1[:, g], ACT.Identity, s["x_norm"])

            def exps(k, l):
                if not here(k):
                    return
                n = seq(k, l)
                act.wait_ge(s["biased"], value(n + 1))
                if some(n):
                    act.wait_ge(s["probs"], value(n))
                for g in range(G):
                    act.activation(EB[:, g], U[:, g], ACT.Exp, bias=bias_b[:, g:g + 1], scale=SLOPE)
                for g in range(G):
                    last = act.activation(U[:, g], U[:, g], ACT.Exp, bias=bias_a[:, g:g + 1])
                last.then_inc(s["exped"], 1)

            def p_high(k, l):
                if not here(k):
                    return
                n = seq(k, l)
                act.wait_ge(s["p_turned"], value(n + 1))
                if some(n * 2):
                    act.wait_ge(s["agg_made"], value(n * 2))
                act.activation(pt_hi[:], ps_s[:], ACT.Copy).then_inc(s["p_hi_made"], 1)

            def ht_high(k, l, d):
                if not here(k):
                    return
                n = seq(k, l) * 2 + d
                act.wait_ge(s["h_turned"], value(n + 1))
                if some(before_last(k, l)):
                    act.wait_ge(s["mm1_made"], value(before_last(k, l) * MC))
                act.activation(ht_hi[:, k % 2, d], ps_ht[:], ACT.Copy).then_inc(s["ht_hi_made"], 1)

            def h0_high(k, half):
                if not here(k):
                    return
                n = k * 2 + half
                act.wait_ge(s["h0_turned"], value(n + 1))
                if some(n):
                    act.wait_ge(s["wh_made"], value(n))
                act.activation(h0_hi[:].rearrange("p c n -> p (c n)"), ps_0[:], ACT.Relu).then_inc(s["h0_hi_made"], 1)

            def wh_high(k, half):
                if not here(k):
                    return
                n = k * 2 + half
                act.wait_ge(s["wh_made"], value(n + 1))
                act.wait_ge(s["e0_made"], value(n + 1))
                if some(k * 2):
                    act.wait_ge(s["z_agg"], value(k * 2))
                act.activation(wh_hi[:, 2 * half:2 * half + 2].rearrange("p g d -> p (g d)"), ps_0[:],
                               ACT.Copy).then_inc(s["wh_hi_made"], 1)

            def z_exps(k):
                if not here(k):
                    return
                act.wait_ge(s["z_biased"], value(k + 1))
                for g in range(G):
                    act.activation(EB0[:, g], U0[:, g], ACT.Exp, bias=zbias_b[:, g:g + 1], scale=SLOPE)
                for g in range(G):
                    last = act.activation(U0[:, g], U0[:, g], ACT.Exp, bias=zbias_a[:, g:g + 1])
                last.then_inc(s["z_exped"], 1)

            def z_high(k):
                if not here(k):
                    return
                act.wait_ge(s["z_turned"], value(k + 1))
                if some(k * 2):
                    act.wait_ge(s["z_agg"], value(k * 2))
                act.activation(pt0_hi[:], ps_0[:], ACT.Copy).then_inc(s["z_hi_made"], 1)

            def elu_exp(k):
                if not here(k):
                    return
                act.wait_ge(s["z_out_made"], value(k * 2 + 2))
                act.activation(UE0[:].rearrange("p a g m -> p (a g m)"), hn0[:].rearrange("p g d -> p (g d)"),
                               ACT.Exp).then_inc(s["elu_exped"], 1)

            def iteration(i):
                for t in range(L):
                    ffn = pair(i, t, 0)
                    att = pair(i, t, -2)
                    mid = pair(i, t, -1)
                    post = pair(i, t, 1)
                    for m in range(MC):
                        gelu(*ffn, m)
                        if m == 0:
                            if t == 1:
                                if peeled(i, -1):
                                    w1_high(2)
                        if m == 2:
                            if t in (0, 2):
                                exps(*att)
                            if t == 1:
                                h_norm(*mid)
                        if m == 3:
                            if t == 1:
                                exps(*att)
                        if m == 4:
                            if t == 0:
                                ht_high(*mid, 0)
                            if t == 1:
                                p_high(*att)
                        if m == 5:
                            if t == 2:
                                ht_high(*mid, 1)
                        if m == 6:
                            if t == 1:
                                h0_high(i + 2, 1)
                        if m == 7:
                            if t == 2:
                                if peeled(i, -2):
                                    w1_high(1)
                        a_high(*ffn, m)
                        if m == 0:
                            if t == 0:
                                h_norm(*mid)
                            if t == 1:
                                x0_norm(i + 2)
                            if t == 2:
                                wh_high(i + 2, 1)
                        if m == 1:
                            if t == 2:
                                if peeled(i, -2):
                                    w2_high(0)
                        if m == 2:
                            if t == 0:
                                elu_exp(i + 1)
                            if t == 1:
                                h0_high(i + 2, 0)
                            if t == 2:
                                z_exps(i + 2)
                                p_high(*att)
                                ht_high(*mid, 0)
                        if m == 3:
                            if t == 0:
                                p_high(*att)
                            if t == 1:
                                ht_high(*mid, 0)
                            if t == 2:
                                if peeled(i, -1):
                                    w2_high(2)
                        if m == 4:
                            if t == 0:
                                y_norm(*post)
                                r_norm(i + 1)
                            if t == 1:
                                wh_high(i + 2, 0)
                                y_norm(*post)
                            if t == 2:
                                y_norm(*post)
                        if m == 5:
                            if t == 1:
                                ht_high(*mid, 1)
                        if m == 6:
                            if t == 0:
                                ht_high(*mid, 1)
                        if m == 7:
                            if t == 1:
                                h_norm(*att)
                                if peeled(i, -2):
                                    w1_high(0)
                            if t == 2:
                                if peeled(i, -2):
                                    w2_high(1)
                                z_high(i + 2)

            schedule(iteration, act)

        @block.vector
        def _(dve):
            stt, tt, ts = dve.scalar_tensor_tensor, dve.tensor_tensor, dve.tensor_scalar

            def w0_parts():
                dve.wait_ge(s["w0_in"], 16)
                dve.tensor_copy(w0_hi[:], w0_stage).then_inc(s["w0_split"], 1)
                dve.wait_ge(s["w0_split"], 1)
                tt(w0_lo[:], w0_stage, w0_hi[:].bitcast(F32), ALU.subtract).then_inc(s["w0_split"], 1)

            def w1_low(l):
                dve.wait_ge(s["w1_hi_made"], l + 1)
                dve.wait_ge(s["w1_biased"], l + 1)
                for d in range(DC):
                    last = stt(out=w1_lo[:, l, d], in0=w1_stage[:, d], scalar=g1_col[:, l, d:d + 1],
                               in1=w1_hi[:, l, d].bitcast(F32), op0=ALU.mult, op1=ALU.subtract)
                last.then_inc(s["w1_split"], 1)

            def biases():
                dve.wait_ge(s["const_in"], 16 * CONSTS)
                tt(bb_row[:].rearrange("p l n -> p (l n)"), bb_row[:].rearrange("p l n -> p (l n)"), b2_row,
                   ALU.add).then_inc(s["bb_made"], 1)
                dve.wait_ge(s["w1_biased"], L)
                b1 = b1_col[:].rearrange("p l m -> p (l m)")
                tt(b1, b1, ps_ht[:, 0:L * MC], ALU.add).then_inc(s["b1_made"], 1)

            def moments(name, n, src):
                st, short = stats[name], name + "st_"
                for g in range(G):
                    last = dve.bn_stats(st["six"][:, g], src(g))
                last.then_inc(s[short + "six"], 1)
                dve.wait_ge(s[short + "six"], value(n + 1))
                settle(dve, s["hold_vector"], n + 1)
                for g in range(G):
                    last = dve.bn_aggr(st["mv"][:, g], st["six"][:, g])
                last.then_inc(s[short + "mv"], 1)
                dve.wait_ge(s[short + "mv"], value(n + 1))
                ts(st["ve"][:], st["mv"][:, :, 1], EPS, None, ALU.add).then_inc(s[short + "ve"], 1)

            def minus_mean(name, k, l=None):
                if not here(k):
                    return
                n = k if l is None else seq(k, l)
                st, short = stats[name], name + "st_"
                dve.wait_ge(s[short + "rstd"], value(n + 1))
                stt(out=st["nmr"][:], in0=st["mv"][:, :, 0], scalar=-1.0, in1=st["rstd"][:],
                    op0=ALU.mult, op1=ALU.mult).then_inc(s[short + "nmr"], 1)

            def x_moments(k):
                if not here(k):
                    return
                dve.wait_ge(s["x_in"], value(k * 16 + 16))
                moments("x", k, lambda g: x1[:, g])

            def r_moments(k):
                if not here(k):
                    return
                dve.wait_ge(s["x1_made"], value(k + 1))
                moments("r", k, lambda g: x1[:, g])

            def masks(k):
                if not here(k):
                    return
                dve.wait_ge(s["adj_in"], value(k * 16 + 16))
                if peeled(k, 0):
                    dve.wait_ge(s["const_made"], 2)
                ts(mask0[:], adj_sb[:], 0.0, OFF, ALU.is_le, ALU.mult).then_inc(s["mask_made"], 1)
                if some(k):
                    dve.wait_ge(s["x1_made"], value(k))
                tt(kept, adj_sb[:], ident[:].rearrange("p (o m) -> p o m", o=1).to_broadcast([P, G, P]),
                   ALU.add).then_inc(s["adj_sum"], 1)
                dve.wait_ge(s["adj_sum"], value(k + 1))
                if some(k * 16):
                    dve.wait_ge(s["mask_parked"], value(k * 16))
                ts(mask_out[:], kept, 0.0, OFF, ALU.is_le, ALU.mult).then_inc(s["mask_made"], 1)

            def h0_low(k, half):
                if not here(k):
                    return
                n = k * 2 + half
                dve.wait_ge(s["h0_hi_made"], value(n + 1))
                if some(n):
                    dve.wait_ge(s["wh_made"], value(n))
                stt(out=h0_lo[:].rearrange("p c n -> p (c n)"), in0=ps_0[:], scalar=0.0,
                    in1=h0_hi[:].rearrange("p c n -> p (c n)").bitcast(F32),
                    op0=ALU.max, op1=ALU.subtract).then_inc(s["h0_split"], 1)

            def wh_scores(k, half):
                if not here(k):
                    return
                n = k * 2 + half
                if isinstance(k, int) and n == 0:
                    dve.wait_ge(s["const_in"], 16 * CONSTS)
                dve.wait_ge(s["wh_made"], value(n + 1))
                if some(k):
                    dve.wait_ge(s["x1_made"], value(k))
                    settle(dve, s["hold_vector"], k)
                for g in range(2):
                    for j in range(2):
                        last = dve.tensor_tensor_reduce(
                            out=junk0[2 * g + j], in0=ps_0[:, g * D:(g + 1) * D], in1=a0_row[:, j], scale=1.0, scalar=0.0,
                            op0=ALU.mult, op1=ALU.add, accum_out=e0[:, j, 2 * half + g:2 * half + g + 1])
                last.then_inc(s["e0_made"], 1)

            def wh_low(k, half):
                if not here(k):
                    return
                n = k * 2 + half
                dve.wait_ge(s["wh_hi_made"], value(n + 1))
                tt(wh_lo[:, 2 * half:2 * half + 2].rearrange("p g d -> p (g d)"), ps_0[:],
                   wh_hi[:, 2 * half:2 * half + 2].rearrange("p g d -> p (g d)").bitcast(F32),
                   ALU.subtract).then_inc(s["wh_split"], 1)

            def z_scores(k):
                if not here(k):
                    return
                dve.wait_ge(s["mask_made"], value(k * 2 + 1))
                settle(dve, s["hold_vector"], k * 2 + 1)
                dve.wait_ge(s["e0_turned"], value(k + 1))
                settle(dve, s["hold_vector"], k + 1)
                if some(k):
                    dve.wait_ge(s["x1_made"], value(k))
                settle(dve, s["hold_vector"], k)
                for g in range(G):
                    last = dve.tensor_tensor_reduce(out=U0[:, g], in0=ps_0[:, g * P:(g + 1) * P], in1=mask0[:, g], scale=1.0,
                                                    scalar=-3e38, op0=ALU.add, op1=ALU.max, accum_out=zmax[:, g:g + 1])
                last.then_inc(s["z_scored"], 1)
                dve.wait_ge(s["z_scored"], value(k + 1))
                tt(zsum[:], zmax[:], e0[:, 0], ALU.add).then_inc(s["z_summed"], 1)
                dve.wait_ge(s["z_summed"], value(k + 1))
                stt(out=zmx[:], in0=zsum[:], scalar=SLOPE, in1=zsum[:], op0=ALU.mult, op1=ALU.max).then_inc(s["z_maxed"], 1)
                dve.wait_ge(s["z_maxed"], value(k + 1))
                tt(zbias_a[:], e0[:, 0], zmx[:], ALU.subtract)
                stt(out=zbias_b[:], in0=e0[:, 0], scalar=SLOPE, in1=zmx[:], op0=ALU.mult,
                    op1=ALU.subtract).then_inc(s["z_biased"], 1)

            def z_probs(k):
                if not here(k):
                    return
                dve.wait_ge(s["z_exped"], value(k + 1))
                for g in range(G):
                    last = stt(out=U0[:, g], in0=U0[:, g], scalar=1.0, in1=EB0[:, g], op0=ALU.mult, op1=ALU.max,
                               accum_out=zden[:, g:g + 1])
                last.then_inc(s["z_probs"], 1)
                dve.wait_ge(s["z_probs"], value(k + 1))
                dve.reciprocal(zrden[:], zden[:]).then_inc(s["z_rden_made"], 1)

            def z_topk(k):
                if not here(k):
                    return
                dve.wait_ge(s["z_probs"], value(k + 1))
                settle(dve, s["hold_vector"], k + 1)
                for g in range(G):
                    last = dve.max(top[:, 0, g], U0[:, g])
                last.then_inc(s["z_top1"], 1)
                dve.wait_ge(s["z_top1"], value(k + 1))
                settle(dve, s["hold_vector"], k + 1)
                for g in range(G):
                    last = dve.match_replace(kept[:, g], top[:, 0, g], U0[:, g], -1.0)
                last.then_inc(s["z_rest"], 1)
                dve.wait_ge(s["z_rest"], value(k + 1))
                settle(dve, s["hold_vector"], k + 1)
                for g in range(G):
                    last = dve.max(top[:, 1, g], kept[:, g])
                last.then_inc(s["z_top2"], 1)
                dve.wait_ge(s["z_top2"], value(k + 1))
                for g in range(G):
                    last = stt(out=U0[:, g], in0=U0[:, g], scalar=top[:, 1, g, 7:8], in1=U0[:, g], op0=ALU.is_ge,
                               op1=ALU.mult)
                last.then_inc(s["z_kept"], 1)

            def z_low(k):
                if not here(k):
                    return
                dve.wait_ge(s["z_hi_made"], value(k + 1))
                if some(k * 2):
                    dve.wait_ge(s["z_agg"], value(k * 2))
                tt(pt0_lo[:], ps_0[:], pt0_hi[:].bitcast(F32), ALU.subtract).then_inc(s["z_split"], 1)

            def z_out(k, half):
                if not here(k):
                    return
                n = k * 2 + half
                dve.wait_ge(s["z_agg"], value(n + 1))
                for g in range(2):
                    last = ts(hn0[:, 2 * half + g], ps_0[:, g * D:(g + 1) * D], zrden[:, 2 * half + g:2 * half + g + 1], None,
                              ALU.mult)
                last.then_inc(s["z_out_made"], 1)

            def elu_plus(k):
                if not here(k):
                    return
                flat = "p g d -> p (g d)"
                dve.wait_ge(s["z_out_made"], value(k * 2 + 2))
                stt(out=x1[:].rearrange(flat), in0=hn0[:].rearrange(flat), scalar=0.0, in1=x1[:].rearrange(flat),
                    op0=ALU.max, op1=ALU.add).then_inc(s["elu_plus"], 1)

            def elu_minus(k):
                if not here(k):
                    return
                e = UE0[:].rearrange("p a g m -> p (a g m)")
                xx = x1[:].rearrange("p g d -> p (g d)")
                dve.wait_ge(s["elu_exped"], value(k + 1))
                ts(e, e, 1.0, -1.0, ALU.min, ALU.add).then_inc(s["elu_minus"], 1)
                dve.wait_ge(s["elu_minus"], value(k + 1))
                tt(xx, xx, e, ALU.add).then_inc(s["x1_made"], 1)

            def x_high(k, l):
                if not here(k):
                    return
                n = seq(k, l)
                dve.wait_ge(s_x[l], value(k + 1))
                if some(n * 2):
                    dve.wait_ge(s["agg_made"], value(n * 2))
                dve.tensor_copy(x_hi[:], X[:, l]).then_inc(s["x_hi_made"], 1)

            def node_scores(k, l):
                if not here(k):
                    return
                n = seq(k, l)
                dve.wait_ge(s_x[l], value(k + 1))
                if some(n):
                    dve.wait_ge(s["p_turned"], value(n))
                    settle(dve, s["hold_vector"], n)
                for g in range(G):
                    for j in range(2):
                        last = dve.tensor_tensor_reduce(
                            out=junk[2 * g + j], in0=X[:, l, g], in1=wij_row[:, l, j], scale=1.0, scalar=0.0,
                            op0=ALU.mult, op1=ALU.add, accum_out=sij[:, l, j, g:g + 1])
                last.then_inc(s["sij_made"], 1)
                dve.wait_ge(s["sij_made"], value(n + 1))
                ts(sib[:, l], sij[:, l, 0], b_att[:, l:l + 1], None, ALU.add).then_inc(s["sib_made"], 1)

            def scores(k, l):
                if not here(k):
                    return
                n = seq(k, l)
                dve.wait_ge(s_mask[l], value(k * 16 + 16))
                settle(dve, s["hold_vector"], k * 16 + 16)
                dve.wait_ge(s["sj_turned"], value(n + 1))
                settle(dve, s["hold_vector"], n + 1)
                if some(n):
                    dve.wait_ge(s["p_turned"], value(n))
                settle(dve, s["hold_vector"], n)
                dve.wait_ge(s["sib_made"], value(n + 1))
                settle(dve, s["hold_vector"], n + 1)
                for g in range(G):
                    last = dve.tensor_tensor_reduce(out=U[:, g], in0=ps_s[:, g * P:(g + 1) * P], in1=mask_in[:, l, g], scale=1.0,
                                                    scalar=-3e38, op0=ALU.add, op1=ALU.max, accum_out=smax[:, g:g + 1])
                last.then_inc(s["scored"], 1)
                dve.wait_ge(s["scored"], value(n + 1))
                tt(ssum[:], smax[:], sib[:, l], ALU.add).then_inc(s["summed"], 1)
                dve.wait_ge(s["summed"], value(n + 1))
                stt(out=smx[:], in0=ssum[:], scalar=SLOPE, in1=ssum[:], op0=ALU.mult, op1=ALU.max).then_inc(s["maxed"], 1)
                dve.wait_ge(s["maxed"], value(n + 1))
                tt(bias_a[:], sib[:, l], smx[:], ALU.subtract)
                stt(out=bias_b[:], in0=sib[:, l], scalar=SLOPE, in1=smx[:], op0=ALU.mult,
                    op1=ALU.subtract).then_inc(s["biased"], 1)

            def probs(k, l):
                if not here(k):
                    return
                n = seq(k, l)
                dve.wait_ge(s["exped"], value(n + 1))
                for g in range(G):
                    last = stt(out=U[:, g], in0=U[:, g], scalar=1.0, in1=EB[:, g], op0=ALU.mult, op1=ALU.max,
                               accum_out=den[:, g:g + 1])
                last.then_inc(s["probs"], 1)
                dve.wait_ge(s["probs"], value(n + 1))
                dve.reciprocal(rden[:], den[:]).then_inc(s["rden_made"], 1)

            def p_low(k, l):
                if not here(k):
                    return
                n = seq(k, l)
                dve.wait_ge(s["p_hi_made"], value(n + 1))
                if some(n * 2):
                    dve.wait_ge(s["agg_made"], value(n * 2))
                tt(pt_lo[:], ps_s[:], pt_hi[:].bitcast(F32), ALU.subtract).then_inc(s["p_split"], 1)

            def y1_sum(k, l, half):
                if not here(k):
                    return
                n = seq(k, l)
                dve.wait_ge(s["rden_made"], value(n + 1))
                dve.wait_ge(s["x_lo_made"], value(n * 2 + half + 1))
                dve.wait_ge(s["agg_made"], value(n * 2 + half + 1))
                for g in range(2):
                    j = 2 * half + g
                    last = stt(out=X[:, l, j], in0=ps_ag[:, g * D:(g + 1) * D], scalar=rden[:, j:j + 1], in1=X[:, l, j],
                               op0=ALU.mult, op1=ALU.add)
                last.then_inc(s["y1_made"], 1)

            def y1_moments(k, l):
                if not here(k):
                    return
                n = seq(k, l)
                dve.wait_ge(s["y1_made"], value(n * 2 + 2))
                moments("h", n, lambda g: X[:, l, g])

            def ht_low(k, l, d):
                if not here(k):
                    return
                n = seq(k, l) * 2 + d
                dve.wait_ge(s["ht_hi_made"], value(n + 1))
                tt(ht_lo[:, k % 2, d], ps_ht[:], ht_hi[:, k % 2, d].bitcast(F32), ALU.subtract).then_inc(s["ht_split"], 1)

            def y_sum(k, l):
                if not here(k):
                    return
                n = seq(k, l)
                dve.wait_ge(s["h_res"], value(n * 2 + 2))
                dve.wait_ge(s["mm2_made"], value(n * MC + MC))
                for half in range(2):
                    h = H[:, k % 2, 2 * half:2 * half + 2].rearrange("p g d -> p (g d)")
                    last = tt(h, ps_ff[half][:], h, ALU.add)
                last.then_inc(s["y_made"], 1)

            def y_moments(k, l):
                if not here(k):
                    return
                n = seq(k, l)
                dve.wait_ge(s["y_made"], value(n + 1))
                moments("y", n, lambda g: H[:, k % 2, g])

            def y_bias(k, l):
                if not here(k):
                    return
                n = seq(k, l)
                dve.wait_ge(s["y_scaled"], value(n * 2 + 2))
                bias = be2_row[:, l:l + 1, :].to_broadcast([P, G, D])
                if l == L - 1:
                    tt(H[:, k % 2], H[:, k % 2], bias, ALU.add).then_inc(s["y_final"], 1)
                    return
                if isinstance(k, int) and seq(k, l) == 0:
                    dve.wait_ge(s["w1_split"], L)
                if not peeled(k, 0):
                    dve.wait_ge(s["h_turned"], value(seq(k - 1, l + 1) * 2 + 2))
                    dve.wait_ge(s["h_scaled"], value(seq(k - 1, l + 1) * 2 + 2))
                tt(X[:, l + 1], H[:, k % 2], bias, ALU.add).then_inc(s_x[l + 1], 1)

            def iteration(i):
                for t in range(L):
                    before = pair(i, t, -3)
                    att = pair(i, t, -2)
                    mid = pair(i, t, -1)
                    post = pair(i, t, 1)
                    done = pair(i, t, 2)
                    for m in range(MC):
                        if m == 0:
                            if t == 0:
                                y_bias(*done)
                                node_scores(*att)
                                minus_mean("h", *mid)
                            if t == 1:
                                y_sum(*post)
                                minus_mean("h", *mid)
                                y_bias(*done)
                            if t == 2:
                                y_bias(*done)
                                if peeled(i, -2):
                                    w1_low(0)
                                minus_mean("h", *mid)
                                node_scores(*att)
                                wh_scores(i + 2, 1)
                                scores(*att)
                        if m == 1:
                            x_high(*att)
                            if t == 0:
                                z_low(i + 1)
                            if t == 1:
                                scores(*att)
                            if t == 2:
                                wh_low(i + 2, 1)
                                y_sum(*post)
                                z_scores(i + 2)
                        if m == 2:
                            if t == 0:
                                scores(*att)
                            if t == 1:
                                h0_low(i + 2, 0)
                            if t == 2:
                                y_moments(*post)
                                probs(*att)
                                if peeled(i, -1):
                                    w1_low(2)
                        if m == 3:
                            if t == 0:
                                y_sum(*post)
                                z_out(i + 1, 0)
                                y_moments(*post)
                                z_out(i + 1, 1)
                                elu_plus(i + 1)
                            if t == 1:
                                y_moments(*post)
                                masks(i + 2)
                                probs(*att)
                                wh_scores(i + 2, 0)
                            if t == 2:
                                z_probs(i + 2)
                        if m == 4:
                            if t == 0:
                                probs(*att)
                                elu_minus(i + 1)
                                minus_mean("y", *post)
                            if t == 1:
                                minus_mean("y", *post)
                                ht_low(*mid, 0)
                                p_low(*att)
                            if t == 2:
                                p_low(*att)
                                ht_low(*mid, 0)
                                minus_mean("y", *post)
                                if peeled(i, -2):
                                    w1_low(1)
                        if m == 5:
                            if t == 0:
                                r_moments(i + 1)
                                if peeled(i, -2):
                                    w0_parts()
                                p_low(*att)
                                if peeled(i, -1):
                                    biases()
                            if t in (1, 2):
                                y1_sum(*att, 0)
                        if m == 6:
                            if t == 0:
                                ht_low(*mid, 0)
                                minus_mean("r", i + 1)
                                y1_sum(*att, 0)
                                node_scores(*before)
                            if t == 1:
                                wh_low(i + 2, 0)
                            if t == 2:
                                z_topk(i + 2)
                                ht_low(*mid, 1)
                        if m == 7:
                            if t == 0:
                                ht_low(*mid, 1)
                                x_moments(i + 2)
                                y1_sum(*att, 1)
                                minus_mean("x", i + 2)
                                y1_moments(*att)
                            if t == 1:
                                y1_sum(*att, 1)
                                y1_moments(*att)
                                ht_low(*mid, 1)
                                h0_low(i + 2, 1)
                            if t == 2:
                                y1_sum(*att, 1)
                                y1_moments(*att)

            schedule(iteration, dve)

        @block.tensor
        def _(pe):
            pe.wait_ge(s["const_made"], 2)

            def three_products(dst, hi, lo, v_hi, v_lo, first, final):
                pe.matmul(dst, hi, v_hi, start=first, stop=False, skip_group_check=True)
                pe.matmul(dst, hi, v_lo, start=False, stop=False, skip_group_check=True)
                return pe.matmul(dst, lo, v_hi, start=False, stop=final, skip_group_check=True)

            def mm1(k, l, m):
                if not here(k):
                    return
                c = seq(k, l) * MC + m
                if m == 0:
                    pe.wait_ge(s["ht_split"], value(seq(k, l) * 2 + 2))
                    if peeled(k, 0):
                        pe.wait_ge(s["w1_split"], l + 1)
                        pe.wait_ge(s["w2_split"], l + 1)
                if some(c - 1):
                    pe.wait_ge(s["gelu_made"], value(c - 1))
                for d in range(DC):
                    cols = slice(m * P, (m + 1) * P)
                    pe.matmul(ps_mm[m % 2][:], w1_hi[:, l, d, cols], ht_hi[:, k % 2, d], start=(d == 0), stop=False)
                    pe.matmul(ps_mm[m % 2][:], w1_lo[:, l, d, cols], ht_hi[:, k % 2, d], start=False, stop=False)
                    last = pe.matmul(ps_mm[m % 2][:], w1_hi[:, l, d, cols], ht_lo[:, k % 2, d], start=False, stop=(d == DC - 1))
                last.then_inc(s["mm1_made"], 1)

            def mm2(k, l, m):
                if not here(k):
                    return
                c = seq(k, l) * MC + m
                if m == 0:
                    if some(seq(k, l)):
                        pe.wait_ge(s["y_made"], value(seq(k, l)))
                pe.wait_ge(s["a_split"], value(c + 1))
                for g in range(G):
                    cols = slice(g * P, (g + 1) * P)
                    last = three_products(ps_ff[g // 2][:, g % 2 * D:(g % 2 + 1) * D], a_hi[:, m % 2, cols], a_lo[:, m % 2, cols],
                                          w2_hi[:, l, m], w2_lo[:, l, m], m == 0 and g % 2 == 0, m == MC - 1 and g % 2 == 1)
                last.then_inc(s["mm2_made"], 1)

            def turn_sj(k, l):
                if not here(k):
                    return
                n = seq(k, l)
                pe.wait_ge(s["sij_made"], value(n + 1))
                if some(n):
                    pe.wait_ge(s["p_split"], value(n))
                for g in range(G):
                    last = pe.transpose(ps_s[:, g * P:(g + 1) * P], sij[:, l, 1, g:g + 1].to_broadcast([P, P]), ident[:])
                last.then_inc(s["sj_turned"], 1)

            def turn_p(k, l):
                if not here(k):
                    return
                n = seq(k, l)
                pe.wait_ge(s["probs"], value(n + 1))
                for g in range(G):
                    last = pe.transpose(ps_s[:, g * P:(g + 1) * P], U[:, g], ident[:])
                last.then_inc(s["p_turned"], 1)

            def agg(k, l, half):
                if not here(k):
                    return
                n = seq(k, l)
                pe.wait_ge(s["p_split"], value(n + 1))
                pe.wait_ge(s["x_lo_made"], value(n * 2 + half + 1))
                if some(n * 2 + half):
                    pe.wait_ge(s["y1_made"], value(n * 2 + half))
                for g in range(2):
                    j = 2 * half + g
                    last = three_products(ps_ag[:, g * D:(g + 1) * D], pt_hi[:, j * P:(j + 1) * P], pt_lo[:, j * P:(j + 1) * P],
                                          x_hi[:, j], x_lo[:, j], g == 0, g == 1)
                last.then_inc(s["agg_made"], 1)

            def turn_h(k, l, d):
                if not here(k):
                    return
                n = seq(k, l) * 2 + d
                pe.wait_ge(s["h_norm"], value(seq(k, l) + 1))
                if some(n):
                    pe.wait_ge(s["ht_split"], value(n))
                if isinstance(k, int) and n == 0:
                    pe.wait_ge(s["b1_made"], 1)
                for g in range(G):
                    last = pe.transpose(ps_ht[:, g * P:(g + 1) * P], X[:, l, g, d * P:(d + 1) * P], ident[:])
                last.then_inc(s["h_turned"], 1)

            def turn_h0(k, half):
                if not here(k):
                    return
                n = k * 2 + half
                pe.wait_ge(s["x_norm"], value(k + 1))
                if some(n):
                    pe.wait_ge(s["wh_split"], value(n))
                if some(k * 2):
                    pe.wait_ge(s["z_out_made"], value(k * 2))
                for d in range(DC):
                    for g in range(2):
                        last = pe.transpose(ps_0[:, (2 * d + g) * P:(2 * d + g + 1) * P],
                                            hn0[:, 2 * half + g, d * P:(d + 1) * P], ident[:])
                last.then_inc(s["h0_turned"], 1)

            def w1_bias(l):
                pe.wait_ge(s_w1[l], 16)
                if l == 0:
                    pe.wait_ge(s["const_in"], 16 * CONSTS)
                for m in range(MC):
                    for d in range(DC):
                        last = pe.matmul(ps_ht[:, l * MC + m:l * MC + m + 1], w1_stage[:, d, m * P:(m + 1) * P],
                                         be1_col[:, l, d:d + 1], start=(l == 0 and m == 0 and d == 0),
                                         stop=(l == L - 1 and m == MC - 1 and d == DC - 1), skip_group_check=True)
                last.then_inc(s["w1_biased"], 1)

            def wh(k, half):
                if not here(k):
                    return
                n = k * 2 + half
                if isinstance(k, int) and n == 0:
                    pe.wait_ge(s["w0_split"], 2)
                pe.wait_ge(s["h0_split"], value(n + 1))
                for g in range(2):
                    for d in range(DC):
                        cols = slice(g * P, (g + 1) * P)
                        last = three_products(ps_0[:, g * D:(g + 1) * D], h0_hi[:, d, cols], h0_lo[:, d, cols],
                                              w0_hi[:, d], w0_lo[:, d], g == 0 and d == 0, g == 1 and d == DC - 1)
                last.then_inc(s["wh_made"], 1)

            def turn_e0(k):
                if not here(k):
                    return
                pe.wait_ge(s["wh_split"], value(k * 2 + 2))
                for g in range(G):
                    last = pe.transpose(ps_0[:, g * P:(g + 1) * P], e0[:, 1, g:g + 1].to_broadcast([P, P]), ident[:])
                last.then_inc(s["e0_turned"], 1)

            def turn_z(k):
                if not here(k):
                    return
                pe.wait_ge(s["z_kept"], value(k + 1))
                for g in range(G):
                    last = pe.transpose(ps_0[:, g * P:(g + 1) * P], U0[:, g], ident[:])
                last.then_inc(s["z_turned"], 1)

            def z_agg(k, half):
                if not here(k):
                    return
                pe.wait_ge(s["z_split"], value(k + 1))
                if some(k * 2 + half):
                    pe.wait_ge(s["z_out_made"], value(k * 2 + half))
                for g in range(2):
                    j = 2 * half + g
                    last = three_products(ps_0[:, g * D:(g + 1) * D], pt0_hi[:, j * P:(j + 1) * P], pt0_lo[:, j * P:(j + 1) * P],
                                          wh_hi[:, j], wh_lo[:, j], g == 0, g == 1)
                last.then_inc(s["z_agg"], 1)

            def iteration(i):
                for t in range(L):
                    ffn = pair(i, t, 0)
                    att = pair(i, t, -2)
                    mid = pair(i, t, -1)
                    post = pair(i, t, 1)
                    for m in range(MC):
                        mm1(*ffn, m)
                        if m == 0:
                            if t == 2:
                                wh(i + 2, 1)
                        if m == 1:
                            if t in (0, 2):
                                turn_sj(*att)
                        if m == 2:
                            if t == 0:
                                z_agg(i + 1, 0)
                            if t == 1:
                                turn_sj(*att)
                                turn_h0(i + 2, 0)
                            if t == 2:
                                turn_e0(i + 2)
                        if m == 3:
                            turn_h(*mid, 0)
                        if m == 4:
                            if t == 0:
                                turn_p(*att)
                            if t == 1:
                                wh(i + 2, 0)
                        if m == 5:
                            if t == 1:
                                turn_p(*att)
                            if t == 2:
                                agg(*att, 1)
                        if m == 6:
                            if t == 0:
                                agg(*att, 0)
                                if peeled(i, -1):
                                    w1_bias(2)
                            if t == 1:
                                agg(*att, 1)
                        if m == 7:
                            if t == 2:
                                turn_z(i + 2)
                        if m < MM2_LAG:
                            mm2(*post, MC - MM2_LAG + m)
                        else:
                            mm2(*ffn, m - MM2_LAG)
                        if m == 2:
                            if t == 0:
                                z_agg(i + 1, 1)
                            if t == 2:
                                if peeled(i, -2):
                                    w1_bias(1)
                        if m == 3:
                            if t == 2:
                                turn_p(*att)
                        if m == 4:
                            if t == 2:
                                agg(*att, 0)
                                turn_h(*mid, 1)
                        if m == 5:
                            if t == 1:
                                turn_h(*mid, 1)
                                agg(*att, 0)
                        if m == 6:
                            if t == 0:
                                turn_h(*mid, 1)
                                agg(*att, 1)
                            if t == 1:
                                turn_h0(i + 2, 1)
                        if m == 7:
                            if t == 1:
                                if peeled(i, -2):
                                    w1_bias(0)

            schedule(iteration, pe)


_INS = ["x", "adj", "L0_gnn_W", "L0_gnn_a", "L1_gnn_attn_w", "L1_gnn_attn_b", "L1_gnn_W1", "L1_gnn_b1",
        "L1_gnn_W2", "L1_gnn_b2", "L1_gnn_g1", "L1_gnn_beta1", "L1_gnn_g2", "L1_gnn_beta2"]


def kernel(**inputs):
    import numpy as np
    import concourse.bacc as bacc
    from concourse import mybir as mb
    from concourse.bass_utils import run_bass_kernel_spmd

    nc = bacc.Bacc("TRN2", target_bir_lowering=False, num_devices=1, dynamic_dma_scratch_size=2048)
    arrays, args = {}, []
    for name in _INS:
        a = np.ascontiguousarray(inputs[name])
        arrays["in_" + name] = a
        args.append(nc.dram_tensor("in_" + name, a.shape, mb.dt.from_np(a.dtype), kind="ExternalInput").ap())
    args.append(nc.dram_tensor("out_0", (B, P, D), F32, kind="ExternalOutput").ap())
    build_program(nc, *args)
    r = run_bass_kernel_spmd(nc, [arrays], core_ids=[0])
    return r.results[0]["out_0"]
```
